# Optimizing a Trainium2 kernel written in Bass

```python
import numpy as np
import jax
import jax.numpy as jnp

def _softmax(x, axis=-1):
    return jax.nn.softmax(x, axis=axis)
def _gelu(x):
    return jax.nn.gelu(x, approximate=True)
def _silu(x):
    return jax.nn.silu(x)
def _sigmoid(x):
    return jax.nn.sigmoid(x)
def _layernorm(x, axis=-1, eps=1e-5):
    m = jnp.mean(x, axis=axis, keepdims=True)
    v = jnp.var(x, axis=axis, keepdims=True)
    return (x - m) / jnp.sqrt(v + eps)
def _scatter_add(tgt, idx, src, axis=0):
    return tgt.at[idx].add(src)
def _segment_sum(src, seg, n):
    return jax.ops.segment_sum(src, seg, n)

kernel_name = 'mk_conv_preact_d2_conv_nchw512_ca8379'

def setup_inputs(seed: int = 0):
    np.random.seed(seed)
    _w = jnp.asarray
    def _rec_inputs():
        import jax
        import jax.numpy as jnp
        _gk = jax.random.key(seed)
        x = -7.109e-05 + 0.9999 * jax.random.normal(jax.random.fold_in(_gk, 1), (32, 512, 64, 64), jnp.float32)
        return x
    x = _rec_inputs()
    def _L0_conv_setup():
        import jax, jax.numpy as jnp
        import numpy as np
        N_QUBITS = 9
        N_LAYERS = 2

        def _quantum_sim(y_pad, q_params):
            b = y_pad.shape[0]
            n = N_QUBITS
            norm = jnp.linalg.norm(y_pad, axis=1, keepdims=True)
            state = y_pad / norm
            state = state.reshape((b,) + (2,) * n)
            for l in range(N_LAYERS):
                for q in range(n):
                    t = q_params[l, q] / 2.0
                    c, s = (jnp.cos(t), jnp.sin(t))
                    ax = q + 1
                    a0 = jnp.take(state, 0, axis=ax)
                    a1 = jnp.take(state, 1, axis=ax)
                    state = jnp.stack([c * a0 - s * a1, s * a0 + c * a1], axis=ax)
                for q in range(n - 1):
                    ax = q + 1
                    c0 = jnp.take(state, 0, axis=ax)
                    c1 = jnp.take(state, 1, axis=ax)
                    c1 = jnp.flip(c1, axis=ax)
                    state = jnp.stack([c0, c1], axis=ax)
            probs = state * state
            zs = []
            for w in range(n):
                other = tuple((a for a in range(1, n + 1) if a != w + 1))
                pw = jnp.sum(probs, axis=other)
                zs.append(pw[:, 0] - pw[:, 1])
            return jnp.stack(zs, axis=1)
        key = jax.random.key(seed)
        k1, k2, k3, k4 = jax.random.split(key, 4)
        b, c, h, w = (32, 512, 64, 64)
        x = jax.random.normal(k1, (b, c, h, w), dtype=jnp.float32)
        q_params = jax.random.normal(k2, (N_LAYERS, N_QUBITS), dtype=jnp.float32) * 0.01
        fan_in = N_QUBITS
        bound = 1.0 / np.sqrt(fan_in)
        fc_w = jax.random.uniform(k3, (c, N_QUBITS), jnp.float32, -bound, bound)
        fc_b = jax.random.uniform(k4, (c,), jnp.float32, -bound, bound)
        return {'x': x, 'q_params': q_params, 'fc_w': fc_w, 'fc_b': fc_b}
    _L0_conv_all = _L0_conv_setup()
    _L0_conv_in = {k: v for k, v in _L0_conv_all.items() if k in ('q_params', 'fc_w', 'fc_b', )}
    del _L0_conv_all

    def _L1_conv_setup():
        import jax, jax.numpy as jnp
        from jax import lax
        import numpy as np
        EPS = 1e-05
        HEADS, DIM_K, R = (4, 16, 15)
        PAD = (R - 1) // 2

        def bn(x, g, b, m, v):
            scale = g * lax.rsqrt(v + EPS)
            return x * scale[None, :, None, None] + (b - m * scale)[None, :, None, None]

        def conv1x1(x, w):
            return jnp.einsum('bchw,oc->bohw', x, w)

        def position_lambdas(emb, values):
            B, V, H, W = values.shape
            vals = values.reshape(B * V, 1, H, W)
            out = lax.conv_general_dilated(vals, emb[:, None, :, :], (1, 1), [(PAD, PAD), (PAD, PAD)])
            out = out.reshape(B, V, DIM_K, H, W).transpose(0, 2, 1, 3, 4)
            return out.reshape(B, DIM_K, V, H * W)

        def lambda_layer(x, q_w, bnq_g, bnq_b, bnq_m, bnq_v, k_w, v_w, bnv_g, bnv_b, bnv_m, bnv_v, emb):
            B, _, H, W = x.shape
            q = bn(conv1x1(x, q_w), bnq_g, bnq_b, bnq_m, bnq_v)
            k = conv1x1(x, k_w)
            v = bn(conv1x1(x, v_w), bnv_g, bnv_b, bnv_m, bnv_v)
            pos = position_lambdas(emb, v)
            k = jax.nn.softmax(k, axis=1)
            dim_v = v.shape[1]
            q = q.reshape(B, HEADS, DIM_K, H * W)
            k = k.reshape(B, DIM_K, H * W)
            v2 = v.reshape(B, dim_v, H * W)
            content_lambda = jnp.einsum('bkm,bvm->bkv', k, v2)
            content_out = jnp.einsum('bhkn,bkv->bhvn', q, content_lambda)
            position_out = jnp.einsum('bhkn,bkvn->bhvn', q, pos)
            out = content_out + position_out
            return out.reshape(B, HEADS * dim_v, H, W)
        key = jax.random.key(seed)
        ks = jax.random.split(key, 32)
        inplanes, width, outplanes = (512, 128, 512)
        dim_v = width // HEADS
        B, H, W = (32, 64, 64)
        n = lambda i, shape, s=1.0: jax.random.normal(ks[i], shape, jnp.float32) * s
        u = lambda i, shape: jax.random.uniform(ks[i], shape, jnp.float32, 0.5, 1.5)
        return {'x': n(0, (B, inplanes, H, W)), 'conv1_w': n(1, (width, inplanes), 0.05), 'bn1_g': u(2, (width,)), 'bn1_b': n(3, (width,), 0.1), 'bn1_m': n(4, (width,), 0.1), 'bn1_v': u(5, (width,)), 'q_w': n(6, (DIM_K * HEADS, width), 0.05), 'bnq_g': u(7, (DIM_K * HEADS,)), 'bnq_b': n(8, (DIM_K * HEADS,), 0.1), 'bnq_m': n(9, (DIM_K * HEADS,), 0.1), 'bnq_v': u(10, (DIM_K * HEADS,)), 'k_w': n(11, (DIM_K, width), 0.05), 'v_w': n(12, (dim_v, width), 0.05), 'bnv_g': u(13, (dim_v,)), 'bnv_b': n(14, (dim_v,), 0.1), 'bnv_m': n(15, (dim_v,), 0.1), 'bnv_v': u(16, (dim_v,)), 'emb': n(17, (DIM_K, R, R), 0.1), 'bn2_g': u(18, (width,)), 'bn2_b': n(19, (width,), 0.1), 'bn2_m': n(20, (width,), 0.1), 'bn2_v': u(21, (width,)), 'conv3_w': n(22, (outplanes, width), 0.05), 'bn3_g': u(23, (outplanes,)), 'bn3_b': n(24, (outplanes,), 0.1), 'bn3_m': n(25, (outplanes,), 0.1), 'bn3_v': u(26, (outplanes,))}
    _L1_conv_all = _L1_conv_setup()
    _L1_conv_in = {k: v for k, v in _L1_conv_all.items() if k in ('conv1_w', 'bn1_g', 'bn1_b', 'bn1_m', 'bn1_v', 'q_w', 'bnq_g', 'bnq_b', 'bnq_m', 'bnq_v', 'k_w', 'v_w', 'bnv_g', 'bnv_b', 'bnv_m', 'bnv_v', 'emb', 'bn2_g', 'bn2_b', 'bn2_m', 'bn2_v', 'conv3_w', 'bn3_g', 'bn3_b', 'bn3_m', 'bn3_v', )}
    del _L1_conv_all

    return {
        "x": x,
        "L0_conv_q_params": _L0_conv_in["q_params"],
        "L0_conv_fc_w": _L0_conv_in["fc_w"],
        "L0_conv_fc_b": _L0_conv_in["fc_b"],
        "L1_conv_conv1_w": _L1_conv_in["conv1_w"],
        "L1_conv_bn1_g": _L1_conv_in["bn1_g"],
        "L1_conv_bn1_b": _L1_conv_in["bn1_b"],
        "L1_conv_bn1_m": _L1_conv_in["bn1_m"],
        "L1_conv_bn1_v": _L1_conv_in["bn1_v"],
        "L1_conv_q_w": _L1_conv_in["q_w"],
        "L1_conv_bnq_g": _L1_conv_in["bnq_g"],
        "L1_conv_bnq_b": _L1_conv_in["bnq_b"],
        "L1_conv_bnq_m": _L1_conv_in["bnq_m"],
        "L1_conv_bnq_v": _L1_conv_in["bnq_v"],
        "L1_conv_k_w": _L1_conv_in["k_w"],
        "L1_conv_v_w": _L1_conv_in["v_w"],
        "L1_conv_bnv_g": _L1_conv_in["bnv_g"],
        "L1_conv_bnv_b": _L1_conv_in["bnv_b"],
        "L1_conv_bnv_m": _L1_conv_in["bnv_m"],
        "L1_conv_bnv_v": _L1_conv_in["bnv_v"],
        "L1_conv_emb": _L1_conv_in["emb"],
        "L1_conv_bn2_g": _L1_conv_in["bn2_g"],
        "L1_conv_bn2_b": _L1_conv_in["bn2_b"],
        "L1_conv_bn2_m": _L1_conv_in["bn2_m"],
        "L1_conv_bn2_v": _L1_conv_in["bn2_v"],
        "L1_conv_conv3_w": _L1_conv_in["conv3_w"],
        "L1_conv_bn3_g": _L1_conv_in["bn3_g"],
        "L1_conv_bn3_b": _L1_conv_in["bn3_b"],
        "L1_conv_bn3_m": _L1_conv_in["bn3_m"],
        "L1_conv_bn3_v": _L1_conv_in["bn3_v"],
    }

def reference(x, L0_conv_q_params, L0_conv_fc_w, L0_conv_fc_b, L1_conv_conv1_w, L1_conv_bn1_g, L1_conv_bn1_b, L1_conv_bn1_m, L1_conv_bn1_v, L1_conv_q_w, L1_conv_bnq_g, L1_conv_bnq_b, L1_conv_bnq_m, L1_conv_bnq_v, L1_conv_k_w, L1_conv_v_w, L1_conv_bnv_g, L1_conv_bnv_b, L1_conv_bnv_m, L1_conv_bnv_v, L1_conv_emb, L1_conv_bn2_g, L1_conv_bn2_b, L1_conv_bn2_m, L1_conv_bn2_v, L1_conv_conv3_w, L1_conv_bn3_g, L1_conv_bn3_b, L1_conv_bn3_m, L1_conv_bn3_v):
    import jax
    import jax.numpy as jnp
    def _L0_conv_ref(x, q_params, fc_w, fc_b):
        import jax, jax.numpy as jnp
        import numpy as np
        N_QUBITS = 9
        N_LAYERS = 2

        def _quantum_sim(y_pad, q_params):
            b = y_pad.shape[0]
            n = N_QUBITS
            norm = jnp.linalg.norm(y_pad, axis=1, keepdims=True)
            state = y_pad / norm
            state = state.reshape((b,) + (2,) * n)
            for l in range(N_LAYERS):
                for q in range(n):
                    t = q_params[l, q] / 2.0
                    c, s = (jnp.cos(t), jnp.sin(t))
                    ax = q + 1
                    a0 = jnp.take(state, 0, axis=ax)
                    a1 = jnp.take(state, 1, axis=ax)
                    state = jnp.stack([c * a0 - s * a1, s * a0 + c * a1], axis=ax)
                for q in range(n - 1):
                    ax = q + 1
                    c0 = jnp.take(state, 0, axis=ax)
                    c1 = jnp.take(state, 1, axis=ax)
                    c1 = jnp.flip(c1, axis=ax)
                    state = jnp.stack([c0, c1], axis=ax)
            probs = state * state
            zs = []
            for w in range(n):
                other = tuple((a for a in range(1, n + 1) if a != w + 1))
                pw = jnp.sum(probs, axis=other)
                zs.append(pw[:, 0] - pw[:, 1])
            return jnp.stack(zs, axis=1)
        b, c, _, _ = x.shape
        y = jnp.mean(x, axis=(2, 3))
        y_pad = jax.lax.stop_gradient(y)
        q_out = _quantum_sim(y_pad, q_params)
        y_excite = jax.nn.sigmoid(q_out @ fc_w.T + fc_b)
        return x * y_excite[:, :, None, None]

    def _L1_conv_ref(x, conv1_w, bn1_g, bn1_b, bn1_m, bn1_v, q_w, bnq_g, bnq_b, bnq_m, bnq_v, k_w, v_w, bnv_g, bnv_b, bnv_m, bnv_v, emb, bn2_g, bn2_b, bn2_m, bn2_v, conv3_w, bn3_g, bn3_b, bn3_m, bn3_v):
        import jax, jax.numpy as jnp
        from jax import lax
        import numpy as np
        EPS = 1e-05
        HEADS, DIM_K, R = (4, 16, 15)
        PAD = (R - 1) // 2

        def bn(x, g, b, m, v):
            scale = g * lax.rsqrt(v + EPS)
            return x * scale[None, :, None, None] + (b - m * scale)[None, :, None, None]

        def conv1x1(x, w):
            return jnp.einsum('bchw,oc->bohw', x, w)

        def position_lambdas(emb, values):
            B, V, H, W = values.shape
            vals = values.reshape(B * V, 1, H, W)
            out = lax.conv_general_dilated(vals, emb[:, None, :, :], (1, 1), [(PAD, PAD), (PAD, PAD)])
            out = out.reshape(B, V, DIM_K, H, W).transpose(0, 2, 1, 3, 4)
            return out.reshape(B, DIM_K, V, H * W)

        def lambda_layer(x, q_w, bnq_g, bnq_b, bnq_m, bnq_v, k_w, v_w, bnv_g, bnv_b, bnv_m, bnv_v, emb):
            B, _, H, W = x.shape
            q = bn(conv1x1(x, q_w), bnq_g, bnq_b, bnq_m, bnq_v)
            k = conv1x1(x, k_w)
            v = bn(conv1x1(x, v_w), bnv_g, bnv_b, bnv_m, bnv_v)
            pos = position_lambdas(emb, v)
            k = jax.nn.softmax(k, axis=1)
            dim_v = v.shape[1]
            q = q.reshape(B, HEADS, DIM_K, H * W)
            k = k.reshape(B, DIM_K, H * W)
            v2 = v.reshape(B, dim_v, H * W)
            content_lambda = jnp.einsum('bkm,bvm->bkv', k, v2)
            content_out = jnp.einsum('bhkn,bkv->bhvn', q, content_lambda)
            position_out = jnp.einsum('bhkn,bkvn->bhvn', q, pos)
            out = content_out + position_out
            return out.reshape(B, HEADS * dim_v, H, W)
        residual = x
        h = jax.nn.relu(bn(conv1x1(x, conv1_w), bn1_g, bn1_b, bn1_m, bn1_v))
        h = lambda_layer(h, q_w, bnq_g, bnq_b, bnq_m, bnq_v, k_w, v_w, bnv_g, bnv_b, bnv_m, bnv_v, emb)
        h = jax.nn.relu(bn(h, bn2_g, bn2_b, bn2_m, bn2_v))
        h = bn(conv1x1(h, conv3_w), bn3_g, bn3_b, bn3_m, bn3_v)
        return jax.nn.relu(h + residual)

    def _gn(v, G=32, eps=1e-5):
        B_, C_, H_, W_ = v.shape
        g = v.reshape(B_, G, C_ // G, H_, W_)
        m = jnp.mean(g, axis=(2, 3, 4), keepdims=True)
        s = jnp.var(g, axis=(2, 3, 4), keepdims=True)
        return ((g - m) / jnp.sqrt(s + eps)).reshape(v.shape)

    def _ln_c(v, eps=1e-6):
        m = jnp.mean(v, axis=1, keepdims=True)
        s = jnp.var(v, axis=1, keepdims=True)
        return (v - m) / jnp.sqrt(s + eps)

    def _ln_t(v, eps=1e-5):
        m = jnp.mean(v, axis=-1, keepdims=True)
        s = jnp.var(v, axis=-1, keepdims=True)
        return (v - m) / jnp.sqrt(s + eps)

    def _to_tokens(v):
        B_, C_, H_, W_ = v.shape
        return v.reshape(B_, C_, H_ * W_).transpose(0, 2, 1)
    def _from_tokens(t, like):
        B_, C_, H_, W_ = like.shape
        return t.transpose(0, 2, 1).reshape(B_, C_, H_, W_)

    x = x + _L0_conv_ref(_gn(x), L0_conv_q_params, L0_conv_fc_w, L0_conv_fc_b)
    x = x + _L1_conv_ref(_gn(x), L1_conv_conv1_w, L1_conv_bn1_g, L1_conv_bn1_b, L1_conv_bn1_m, L1_conv_bn1_v, L1_conv_q_w, L1_conv_bnq_g, L1_conv_bnq_b, L1_conv_bnq_m, L1_conv_bnq_v, L1_conv_k_w, L1_conv_v_w, L1_conv_bnv_g, L1_conv_bnv_b, L1_conv_bnv_m, L1_conv_bnv_v, L1_conv_emb, L1_conv_bn2_g, L1_conv_bn2_b, L1_conv_bn2_m, L1_conv_bn2_v, L1_conv_conv3_w, L1_conv_bn3_g, L1_conv_bn3_b, L1_conv_bn3_m, L1_conv_bn3_v)
    return x


_drawn_inputs = setup_inputs


def setup_inputs(seed=0):
    import zlib

    import numpy as np

    out = dict(_drawn_inputs(seed))
    spreads = {}
    factors = {'L0_conv_q_params': 37.825,
     'L0_conv_fc_w': 8.0,
     'L1_conv_emb': 5.749,
     'L1_conv_bn2_b': 64.0,
     'L1_conv_bn2_m': 64.0,
     'L1_conv_bn3_b': 56.112,
     'L1_conv_bn3_m': 50.229}
    for name, (base, spread) in spreads.items():
        noise = np.random.default_rng([zlib.crc32(name.encode()), seed]).standard_normal(out[name].shape)
        drawn = base * np.exp(spread * noise) if base else spread * noise
        out[name] = jnp.asarray(drawn.astype(out[name].dtype))
    for name, factor in factors.items():
        out[name] = (out[name] * factor).astype(out[name].dtype)
    return out
```

```python
from contextlib import ExitStack

import concourse.bass as bass
import concourse.mybir as mybir
import numpy as np

F32 = mybir.dt.float32
BF16 = mybir.dt.bfloat16
ALU = mybir.AluOpType
ACT = mybir.ActivationFunctionType
AXX = mybir.AxisListType.X

P = 128
NB, C, HW = 32, 512, 4096
CC = C // P
GRP = 16
NU, UN = 8, 512
PAIRS = NU // 2
SLOTS = 12
SLOT = CC * UN
WD = 128
HD, DK, DV, R = 4, 16, 32, 15
NQ = 9
WROWS, WCM, WCD = 6, 4, 5
WP = WROWS * WCM * WCD
VROWS, VXD = 78, 20
VROW = WCM * VXD * DV
EPR, EPC = 21, 24
NP = 12
GN_EPS0 = 1e-5
BN_EPS = 1e-5
QPART = DK * HD * UN
TWO_PI = 6.283185307179586
MAGIC = 12582912.0


def build(nc, x, bnp, w1, w3, wq, wkv, emb, qpar, fcw, fcb, kbit, gbit, sign, ident, gavg, mask, rep, out):
    ctx = ExitStack()
    with ctx:
        def sb(name, shape, dt=F32):
            return ctx.enter_context(nc.sbuf_tensor(name, shape, dt))

        def pb(name):
            return ctx.enter_context(nc.psum_tensor(name, [P, 512], F32))

        def sem(name):
            return ctx.enter_context(nc.semaphore(name))

        vpad = nc.dram_tensor("vpad", [VROWS * VROW], F32, kind="Internal").ap()
        qparts_d = nc.dram_tensor("qparts_d", [NU * 3 * QPART], BF16, kind="Internal").ap()

        zmove = nc.dram_tensor("zmove", [2 * P * 512], F32, kind="Internal").ap()

        xr = sb("xr", [P, SLOTS * SLOT])
        pw = sb("pw", [P, 2, 32, 64])
        win = sb("win", [P, 2, 6 * 512])
        e8 = sb("e8", [P, 48, WP], BF16)
        ut = sb("ut", [P, CC, C])
        h1 = sb("h1", [P, 2, UN])
        qf = sb("qf", [P, UN])
        qp = sb("qp", [P, 3, UN], BF16)
        q8 = sb("q8", [P, 2, HD, UN], BF16)
        z1 = sb("z1", [P, 2, HD, P])
        z = sb("z", [P, 2, UN])
        t = sb("t", [P, 2, UN])
        w1t = sb("w1t", [P, CC, P])
        w1s = sb("w1s", [P, CC, P])
        w3t = sb("w3t", [P, C])
        wqt = sb("wqt", [P, HD * DK])
        wkvt = sb("wkvt", [P, DV + DK])
        bvb = sb("bvb", [P, DV])
        kt = sb("kt", [P, 32, DK])
        kmx = sb("kmx", [P, 32])
        ksum = sb("ksum", [P, 32])
        vt = sb("vt", [P, 32, DV])
        cls = sb("cls", [DK, DV])
        clf = sb("clf", [P, 3, DV])
        clh = sb("clh", [P, 3, DV], BF16)
        cl8 = sb("cl8", [P, DV], BF16)
        st = sb("st", [P, CC, NU, 6])
        g = sb("g", [P, 30, CC])
        coef = sb("coef", [P, 3, CC])
        bias1 = sb("bias1", [P, 1])
        bn = sb("bn", [P, 4, 8])
        bsc = sb("bsc", [P, 8])
        bsh = sb("bsh", [P, 8])
        half = sb("half", [P, 8])
        zero_s = sb("zero_s", [P, 1])
        fcw_s = sb("fcw_s", [NQ, C])
        fcb_s = sb("fcb_s", [P, CC])
        sign_s = sb("sign_s", [P, CC, NQ])
        id_s = sb("id_s", [P, P])
        gavg_s = sb("gavg_s", [P, P])
        mask_s = sb("mask_s", [P, 3])
        rep_s = sb("rep_s", [DK, P])
        ones9 = sb("ones9", [P, NQ])

        pwf = pw[:, :, :, :].rearrange("p a b c -> p (a b c)")
        winf = win[:, :, :].rearrange("p a b -> p (a b)")
        m0 = pwf[:, 0:2048].rearrange("p (c j) -> p c j", c=CC)
        g1 = pwf[:, 2048:4096].rearrange("p (c i) -> p c i", c=CC)
        w1n, w3n = winf[:, 0:512], winf[:, 512:1024]
        wqn, wkvn = winf[0:64, 1024:1152], winf[0:48, 1152:1280]
        ep = winf[:, 1280:1280 + EPR * EPC]
        er = winf[:, 1792:1792 + EPR * EPC]
        embn = winf[:, 2304:2304 + R * R]
        tvb = winf[0:DV, 2560:2560 + P]
        skv = winf[0:48, 2688:2689]
        ang = winf[:, 2700:2736]
        angn = winf[:, 2740:2776]
        bits = winf[:, 2780:2780 + 36].rearrange("p (c q) -> p c q", c=CC)
        gits = winf[:, 2820:2820 + 36].rearrange("p (c q) -> p c q", c=CC)
        al = winf[:, 2860:2860 + 4 * 36].rearrange("p (m c q) -> p m c q", m=4, c=CC)
        nbit = winf[:, 3004:3004 + 36].rearrange("p (c q) -> p c q", c=CC)
        dbl = [h1[:, 0, :], h1[:, 1, :]]
        eh = q8[:, 0, :, :].rearrange("p a b -> p (a b)")
        ehp = [eh[:, i * 512:i * 512 + EPR * EPC] for i in range(3)]
        ep8 = eh[:, 1536:1536 + EPR * EPC]

        PB = [pb(f"PB{i}") for i in range(3)]
        SM = pb("SM")
        VO = [pb(f"VO{i}") for i in range(2)]
        CO = [pb(f"CO{i}") for i in range(2)]

        s_in = sem("s_in")
        s_zero = sem("s_zero")
        s_set = sem("s_set")
        s_scl = sem("s_scl")
        s_trig = sem("s_trig")
        s_spe = sem("s_spe")
        s_x = [sem(f"s_x{i}") for i in range(2)]
        s_st = [sem(f"s_st{i}") for i in range(2)]
        s_bs = sem("s_bs")
        s_gd = sem("s_gd")
        s_gv = sem("s_gv")
        s_gx = sem("s_gx")
        s_gb = sem("s_gb")
        s_gp = sem("s_gp")
        s_gl = sem("s_gl")
        s_ge = sem("s_ge")
        s_dcs = sem("s_dcs")
        s_dc = sem("s_dc")
        s_km = sem("s_km")
        s_conv = sem("s_conv")
        s_h1 = sem("s_h1")
        s_kv = sem("s_kv")
        s_q = sem("s_q")
        s_qf = sem("s_qf")
        s_pc = sem("s_pc")
        s_qw = sem("s_qw")
        s_kvev = sem("s_kvev")
        s_ex = sem("s_ex")
        s_vw = sem("s_vw")
        s_sc = sem("s_sc")
        s_lc = sem("s_lc")
        s_kn = sem("s_kn")
        s_cl = sem("s_cl")
        s_clc = sem("s_clc")
        s_q8 = [sem(f"s_q8{i}") for i in range(2)]
        s_win = [sem(f"s_win{i}") for i in range(2)]
        s_p = sem("s_p")
        s_pev = sem("s_pev")
        s_vst = sem("s_vst")
        s_vo = sem("s_vo")
        s_vev = sem("s_vev")
        s_zd = [sem(f"s_zd{i}") for i in range(2)]
        s_z = [sem(f"s_z{i}") for i in range(2)]
        s_zr = sem("s_zr")
        s_c3 = sem("s_c3")
        s_co = sem("s_co")
        s_t = sem("s_t")
        s_fin = sem("s_fin")
        s_cf = sem("s_cf")

        N_IN = 17
        block = ctx.enter_context(nc.Block())

        def wait_each(eng, *waits):
            values = [n if isinstance(n, int) else eng.snap(eng.to_reg(n)) for _, n in waits]
            for (s, _), n in zip(waits, values):
                eng.wait_ge(s, n)

        def pick(v, link, f, parts, out, last=None):
            link(v.tensor_scalar(f, parts[0], mask_s[:, 0:1], None, ALU.mult))
            link(v.scalar_tensor_tensor(f, parts[1], mask_s[:, 1:2], f, ALU.mult, ALU.add))
            ins = v.scalar_tensor_tensor(out, parts[2], mask_s[:, 2:3], f, ALU.mult, ALU.add)
            if last:
                ins.then_inc(*last)
            else:
                link(ins)

        def xs(b, u, oc):
            return xr[:, bass.ds(((b * NU + u) % SLOTS) * SLOT + oc * UN, UN)]

        def xslot(b, u):
            return xr[:, bass.ds(((b * NU + u) % SLOTS) * SLOT, SLOT)].rearrange("p (c n) -> p c n", c=CC)

        x_v = x.rearrange("b (c p) n -> b p c n", p=P)
        out_v = out.rearrange("b (c p) n -> b p c n", p=P)

        def dram_unit(v, b, u):
            return v[bass.ds(b, 1), :, :, bass.ds(u * UN, UN)].rearrange("b p c n -> (b p) c n")

        @block.sync
        def _(sp):
            for dst, src in ((bn[:, :, :], bnp), (w1n, w1), (w3n.rearrange("p (c v) -> p c v", c=CC),
                             w3.rearrange("(c p) v -> p c v", p=P)), (wqn, wq), (wkvn, wkv), (embn, emb),
                             (ang[:, 0:18], qpar), (ang[:, 18:36], qpar), (bits, kbit), (gits, gbit),
                             (fcw_s[:, :], fcw), (fcb_s[:, :], fcb), (sign_s[:, :, :], sign),
                             (id_s[:, :], ident), (gavg_s[:, :], gavg), (mask_s[:, :], mask),
                             (rep_s[:, :], rep)):
                sp.dma_start(dst, src).then_inc(s_in, 16)

            def load_x(b, k, par):
                sp.dma_start(xslot(b, k), dram_unit(x_v, b, k)).then_inc(s_x[par], 16)

            for k in range(NU):
                if k >= 2:
                    sp.wait_ge(s_x[k % 2], 16 * (k // 2))
                load_x(0, k, k % 2)
            sp.wait_ge(s_set, 1)
            flat = t[:, :, :].rearrange("p a b -> p (a b)")
            body = VROWS * VROW // P
            vz = vpad.rearrange("(p n) -> p n", p=P)
            for o in range(0, body, 1024):
                n = min(1024, body - o)
                sp.dma_start(vz[:, o:o + n], flat[:, 0:n]).then_inc(s_zero, 16)
            sp.wait_ge(s_zero, 16 * (-(-body // 1024)))

            def z_load(b, u, par, cnt):
                sp.wait_ge(s_zd[par], 16 * (cnt + 1))
                src = bass.AP(zmove.tensor, par * (P * 512), [[P, P], [DV * 512, 4], [1, P]])
                sp.dma_start(z[:, par, :].rearrange("p (j n) -> p j n", j=4), src).then_inc(s_z[par], 16)

            def q8_load(u, par):
                for lo, n, part in ((0, 3, 0), (48, 3, 1), (96, 2, 2)):
                    src = bass.AP(qparts_d.tensor, u * (3 * QPART) + part * QPART, [[0, n], [HD * UN, DK], [1, HD * UN]])
                    sp.dma_start(q8[lo:lo + DK * n, par, :, :].rearrange("p h n -> p (h n)"), src
                                 ).then_inc(s_q8[par], 16)

            def win_load(u, par):
                dst = win[:, par, :].rearrange("p (c y n) -> p c y n", c=3, y=2)
                for yb in range(2):
                    for cd in range(WCD):
                        src = bass.AP(vpad.tensor, u * (8 * VROW) + (4 * yb * VROW + cd * DV),
                                      [[VXD * DV, WROWS * WCM], [WROWS * VROW, 3], [1, 512]])
                        sp.dma_start(dst[cd * 24:cd * 24 + 24, :, yb, :], src).then_inc(s_win[par], 16)

            def v_store(a):
                for r in range(8):
                    dst = bass.AP(vpad.tensor, a * (16 * VROW) + (7 * VROW + 2 * DV + r * VXD * DV),
                                  [[DV, 16], [2 * VROW, 8], [1, DV]])
                    sp.dma_start(dst, vt[16 * r:16 * r + 16, bass.ds(a * 8, 8), :]).then_inc(s_vw, 16)

            def q_store(a):
                for i in range(2):
                    dst = bass.AP(qparts_d.tensor, a * (6 * QPART) + i * 3 * QPART, [[UN, HD * DK], [QPART, 3], [1, UN]])
                    sp.dma_start(dst, qp[64 * i:64 * i + 64, :, :]).then_inc(s_qw, 16)

            def pair_stores(b, a):
                pi = b * PAIRS + a
                wait_each(sp, (s_vw, 128 * pi), (s_kvev, 2 * (pi + 1)))
                v_store(a)
                wait_each(sp, (s_qw, 32 * pi), (s_pc, 5 * (pi + 1)))
                q_store(a)

            def stored(b, a):
                wait_each(sp, (s_vw, 128 * (b * PAIRS + a + 1)), (s_qw, 32 * (b * PAIRS + a + 1)))

            def phase_a(b, prev):
                if prev:
                    sp.wait_ge(s_vev, 2 + b * NU)
                    z_load(b - 1, NU - 1, 1, (b - 1) * 4 + 3)
                pair_stores(b, 0)
                stored(b, 0)
                q8_load(0, 0)
                q8_load(1, 1)
                win_load(0, 0)
                pair_stores(b, 1)
                stored(b, 1)
                win_load(1, 1)
                with sp.Fori(2, PAIRS) as a:
                    pair_stores(b, a)

            def load_next(b, h, par):
                wait_each(sp, (s_x[par], 16 * (b * 4 + h + 5)), (s_st[par], 16 * (b * 4 + h)))
                load_x(b + 1, 2 * h + 2 + par, par)

            def unit(b, u, par, cnt, load, ahead=True):
                sp.wait_ge(s_vev, 2 + b * NU + u)
                if ahead:
                    q8_load(u + 1, 1 - par)
                    win_load(u + 1, 1 - par)
                z_load(b, u - 1, 1 - par, cnt - (1 - par))
                if load:
                    load()

            def sample(b, last):
                n = 16 * PAIRS * (b + 1)
                wait_each(sp, (s_vw, 8 * n), (s_qw, 2 * n))
                if not last:
                    wait_each(sp, (s_st[0], 64 * b), (s_st[1], 64 * b), (s_x[0], n), (s_x[1], n))
                    for k in range(2):
                        load_x(b + 1, k, k)
                unit(b, 1, 1, b * 4, None)
                if not last:
                    load_next(b, 0, 0)
                    load_next(b, 0, 1)
                with sp.Fori(1, 3) as w:
                    unit(b, 2 * w, 0, b * 4 + w, None if last else (lambda: load_next(b, w, 0)))
                    unit(b, 2 * w + 1, 1, b * 4 + w, None if last else (lambda: load_next(b, w, 1)))
                unit(b, 6, 0, b * 4 + 3, None)
                unit(b, 7, 1, b * 4 + 3, None, ahead=False)

            phase_a(0, False)
            with sp.Fori(0, NB - 1) as b:
                sample(b, False)
                phase_a(b + 1, True)
            sample(NB - 1, True)
            z_load(NB - 1, NU - 1, 1, (NB - 1) * 4 + 3)
            sp.wait_ge(s_st[0], 16 * NB * 4)
            sp.wait_ge(s_st[1], 16 * NB * 4)

        @block.tensor
        def _(pe):
            mm = nc.tensor.matmul
            pe.wait_ge(s_set, 3)
            for oc in range(CC):
                nc.tensor.transpose(PB[0][:, oc * P:(oc + 1) * P], w1n[:, oc * P:(oc + 1) * P], id_s[:, :])
            for oc in range(CC):
                nc.tensor.transpose(PB[1][:, oc * P:(oc + 1) * P], w3n[:, oc * P:(oc + 1) * P], id_s[:, :])
            nc.tensor.transpose(PB[2][:, 0:64], wqn, id_s[0:64, 0:64])
            nc.tensor.transpose(PB[2][:, 64:112], wkvn, id_s[0:48, 0:48])
            mm(PB[2][:, 128:160], tvb, id_s[0:DV, 0:DV], start=True, stop=True).then_inc(s_spe, 1)
            pe.wait_ge(s_set, 4)
            for jc in range(CC):
                o = (CO + VO)[jc]
                for kc in range(CC):
                    last = mm(o[:, :], m0[:, kc, jc * P:(jc + 1) * P], g1[:, kc, :], start=kc == 0, stop=kc == CC - 1)
                    if jc == CC - 1 and kc in (1, 2):
                        last.then_inc(s_vst, 1)
            last.then_inc(s_spe, 1)

            def gstep(b, n):
                pe.wait_ge(s_gd, 8 * b + n)
                if n in (1, 2, 6, 7):
                    col, src = {1: (0, 0), 2: (4, 3), 6: (18, 17), 7: (22, 20)}[n]
                    rhs = mean_ap if n == 1 else g[:, src, :]
                    last = mm(SM[:, col:col + 4], gavg_s[:, :], rhs, start=True, stop=True)
                elif n == 3:
                    for ic in range(CC):
                        for jc in range(CC):
                            last = mm(SM[:, 8 + ic:9 + ic], ut[:, jc, ic * P:(ic + 1) * P], g[:, 6, jc:jc + 1],
                                      start=jc == 0, stop=jc == CC - 1)
                elif n == 4:
                    for jc in range(CC):
                        mm(SM[0:NQ, 12:13], sign_s[:, jc, :], g[:, 9, jc:jc + 1], start=jc == 0, stop=jc == CC - 1)
                    for jc in range(CC):
                        last = mm(SM[0:NQ, 13:14], ones9[:, :], g[:, 7, jc:jc + 1], start=jc == 0, stop=jc == CC - 1)
                elif n == 5:
                    for oc in range(CC):
                        last = mm(SM[:, 14 + oc:15 + oc], fcw_s[:, oc * P:(oc + 1) * P], g[0:NQ, 11, 0:1],
                                  start=True, stop=True)
                else:
                    for oc in range(CC):
                        last = mm(SM[:, 26:27], w1t[:, oc, :], g[:, 24, oc:oc + 1], start=oc == 0, stop=oc == CC - 1)
                last.then_inc(s_gp, 1)

            def conv3(b, u, par):
                U = b * NU + u
                pe.wait_ge(s_zr, U + 1)
                for oc in range(CC):
                    pe.wait_ge(s_co, 4 * U + oc + 1)
                    mm(CO[oc % 2][:, :], w3t[:, oc * P:(oc + 1) * P],
                       z[:, par, :].rearrange("p (j y c) -> p y j c", j=4, y=8), start=True, stop=True
                       ).then_inc(s_c3, 1)

            def pair(b, a):
                pi = b * PAIRS + a
                for i in range(2):
                    for k in range(CC):
                        last = mm(CO[i][:, :], w1s[:, k, :], xs(b, 2 * a + i, k), start=k == 0, stop=k == CC - 1)
                    last.then_inc(s_conv, 1)

                def keys_values(i):
                    pe.wait_ge(s_h1, 2 * pi + i + 1)
                    pe.wait_ge(s_kvev, 2 * pi)
                    for n in range(4):
                        last = mm(PB[i][:, n * 48:(n + 1) * 48], h1[:, i, n * P:(n + 1) * P], wkvt[:, :],
                                  start=True, stop=True)
                    last.then_inc(s_kv, 1)

                keys_values(0)
                pe.wait_ge(s_h1, 2 * pi + 2)
                pe.wait_ge(s_qf, pi)
                mm(VO[0][0:64, :], wqt[:, :], h1[:, 0, :], start=True, stop=True)
                mm(VO[0][64:128, :], wqt[:, :], h1[:, 1, :], start=True, stop=True).then_inc(s_q, 1)
                keys_values(1)

            def phase_a(b, prev):
                pe.wait_ge(s_gd, 8 * b + 8)
                if prev:
                    pe.wait_ge(s_co, 2 + 4 * (b * NU - 1))
                pair(b, 0)
                if prev:
                    conv3(b - 1, NU - 1, 1)
                with pe.Fori(1, PAIRS) as a:
                    pe.wait_ge(s_co, 2 + 4 * b * NU)
                    pair(b, a)

            def p_stage(b, u, par, c):
                for oy in range(4):
                    f = 4 * c + oy
                    pe.wait_ge(s_pev, NP * (b * NU + u) + f + 1)
                    qv = q8[:, par, :, :].rearrange("p h (y r m d) -> p h y r m d", y=2, r=4, m=4)
                    for ox in range(4):
                        last = mm(PB[f % 3][0:WP, ox * P:(ox + 1) * P], e8[:, (oy * 4 + ox) * 3 + c, :],
                                  qv[:, :, :, oy, ox, :], start=True, stop=True)
                    last.then_inc(s_p, 1)

            def v_stage(b, u, par, c):
                U = b * NU + u
                pe.wait_ge(s_pev, 3 + NP * U + 4 * c + 4)
                for yb in range(2):
                    for xl in range(4):
                        for j in range(4):
                            xb = 4 * j + xl
                            o = VO[par][32 * j:32 * j + 32, :].rearrange("p (h y r c) -> p h y r c", h=HD, y=2, r=4)
                            last = mm(o[:, :, yb, :, 4 * xl:4 * xl + 4],
                                      win[0:WP, par, ((c * 2 + yb) * 16 + xb) * DV:((c * 2 + yb) * 16 + xb + 1) * DV],
                                      pw[0:WP, (par * 3 + c) % 2, yb * 16 + xb, :],
                                      start=c == 0 and yb == 0 and xl == 0, stop=False, skip_group_check=True)
                last.then_inc(s_vst, 1)

            def content(b, u, par):
                for h in range(HD):
                    for j in range(4):
                        qv = q8[:, par, h, :].rearrange("p (y m d) -> p y d m", y=8, m=4)
                        last = mm(VO[par][32 * j:32 * j + 32, h * P:(h + 1) * P], cl8[:, :],
                                  qv[:, :, 4 * j:4 * j + 4, :], start=False, stop=True, skip_group_check=True)
                last.then_inc(s_vo, 1)

            def unit(b, w, par, middle, after=None, gs=False):
                u, cnt = 2 * w + par, b * 4 + w
                U = b * NU + u
                step = (lambda k: gstep(b + 1, k)) if gs else (lambda k: None)
                pe.wait_ge(s_q8[par], 48 * (cnt + 1))
                p_stage(b, u, par, 0)
                step(1)
                p_stage(b, u, par, 1)
                step(2)
                pe.wait_ge(s_win[par], 160 * (cnt + 1))
                pe.wait_ge(s_vev, U + 1)
                v_stage(b, u, par, 0)
                step(3)
                p_stage(b, u, par, 2)
                step(4)
                v_stage(b, u, par, 1)
                step(5)
                if after:
                    middle()
                v_stage(b, u, par, 2)
                if after:
                    after()
                content(b, u, par)
                if not after:
                    middle()
                for k in (6, 7, 8):
                    step(k)

            def sample(b, last):
                pe.wait_ge(s_kvev, NU * (b + 1))
                pe.wait_ge(s_qf, PAIRS * (b + 1))

                def lambdas():
                    pe.wait_ge(s_kn, b + 1)
                    for n in range(32):
                        last = mm(SM[0:DK, 32:64], kt[:, n, :], vt[:, n, :], start=n == 0, stop=n == 31)
                    last.then_inc(s_cl, 1)

                def spread():
                    pe.wait_ge(s_clc, 2 * b + 1)
                    mm(SM[:, 64:96], rep_s[:, :], cls[:, :], start=True, stop=True).then_inc(s_cl, 1)
                    pe.wait_ge(s_clc, 2 * b + 2)

                unit(b, 0, 0, middle=lambdas, after=spread)
                unit(b, 0, 1, middle=lambda: conv3(b, 0, 0))
                with pe.Fori(1, 3) as w:
                    unit(b, w, 0, middle=lambda: conv3(b, 2 * w - 1, 1))
                    unit(b, w, 1, middle=lambda: conv3(b, 2 * w, 0))
                unit(b, 3, 0, middle=lambda: conv3(b, 5, 1))
                unit(b, 3, 1, middle=lambda: conv3(b, 6, 0), gs=not last)

            mean_ap = g[:, 0:2, :].rearrange("p a b -> p (a b)")[:, 0:8:2]
            for k in range(1, 9):
                gstep(0, k)
            phase_a(0, False)
            with pe.Fori(0, NB - 1) as b:
                sample(b, False)
                phase_a(b + 1, True)
            sample(NB - 1, True)
            conv3(NB - 1, NU - 1, 1)

        @block.scalar
        def _(act):
            act.wait_ge(s_set, 2)
            nc.scalar.activation(angn, ang, ACT.Sin).then_inc(s_trig, 1)

            act.wait_ge(s_spe, 1)
            for i, (dst, src) in enumerate(((w1t[:, :, :].rearrange("p c o -> p (c o)"), PB[0][:, :]),
                                            (w3t[:, :], PB[1][:, :]), (wqt[:, :], PB[2][:, 0:64]),
                                            (wkvt[:, :], PB[2][:, 64:112]), (bvb[:, :], PB[2][:, 128:160]))):
                ins = nc.scalar.activation(dst, src, ACT.Copy)
                if i in (0, 1, 4):
                    ins.then_inc(s_pev, 1)

            def z_relu(b, u, par, cnt):
                act.wait_ge(s_z[par], 16 * (cnt + 1))
                nc.scalar.activation(z[:, par, :], z[:, par, :], ACT.Relu, bias=bsh[:, 2:3], scale=bsc[:, 2:3]
                                     ).then_inc(s_zr, 1)

            def pair(b, a, prev):
                pi = b * PAIRS + a
                for i in range(2):
                    act.wait_ge(s_conv, 2 * pi + i + 1)
                    nc.scalar.activation(h1[:, i, :].rearrange("p (y m d) -> p y d m", y=8, m=4),
                                         CO[i][:, :].rearrange("p (y d m) -> p y d m", y=8, m=4),
                                         ACT.Relu, bias=bias1[:, :]).then_inc(s_h1, 1)
                for i in range(2):
                    for oc in range(CC):
                        nc.scalar.activation(xs(b, 2 * a + i, oc), xs(b, 2 * a + i, oc), ACT.Copy,
                                             scale=g[:, 16, oc:oc + 1])
                act.wait_ge(s_q, pi + 1)
                act.wait_ge(s_pc, 5 * pi)
                nc.scalar.activation(qf[:, :], VO[0][:, :], ACT.Identity, bias=bsh[:, 1:2]).then_inc(s_qf, 1)
                if prev:
                    z_relu(b - 1, NU - 1, 1, (b - 1) * 4 + 3)
                act.wait_ge(s_kvev, 2 * pi + 2)
                kp = kt[:, bass.ds(a * 8, 8), :]
                nc.scalar.activation(kp, kp, ACT.Exp).then_inc(s_ex, 1)

            def phase_a(b, prev):
                act.wait_ge(s_gb, b + 1)
                pair(b, 0, prev)
                with act.Fori(1, PAIRS) as a:
                    pair(b, a, False)

            def p_copy(b, u, par, c):
                U = b * NU + u
                act.wait_ge(s_vst, 3 * U + c + 1)
                for oy in range(4):
                    f = 4 * c + oy
                    act.wait_ge(s_p, NP * U + f + 1)
                    dst = pw[0:WP, (par * 3 + c) % 2, :, :].rearrange("p k (h r o) -> p r o h k", h=HD, r=4)
                    nc.scalar.activation(dst[:, oy], PB[f % 3][0:WP, :].rearrange("p (o h k) -> p o h k", o=4, h=HD),
                                         ACT.Copy).then_inc(s_pev, 1)

            def unit(b, u, par, cnt, zr=True, ge=False):
                U = b * NU + u
                p_copy(b, u, par, 0)
                p_copy(b, u, par, 1)
                p_copy(b, u, par, 2)
                if zr:
                    z_relu(b, u - 1, 1 - par, cnt - (1 - par))
                if ge:
                    gate(b + 1)
                act.wait_ge(s_vo, U + 1)
                act.wait_ge(s_z[par], 16 * cnt)
                nc.scalar.activation(z1[:, par, :, :].rearrange("p h n -> p (h n)"), VO[par][:, :], ACT.Copy
                                     ).then_inc(s_vev, 1)
                act.wait_ge(s_vev, U + 3)
                act.dma_start(bass.AP(zmove.tensor, par * (P * 512), [[512, P], [1, 512]]),
                              z1[:, par, :, :].rearrange("p h n -> p (h n)")).then_inc(s_zd[par], 16)

            def gate(b):
                act.wait_ge(s_gx, b + 1)
                nc.scalar.activation(g[:, 13, :], g[:, 12, :], ACT.Exp, scale=-1.0).then_inc(s_ge, 1)

            def sample(b, last):
                unit(b, 0, 0, b * 4, zr=False)
                unit(b, 1, 1, b * 4)
                with act.Fori(1, 3) as w:
                    for i in range(2):
                        unit(b, 2 * w + i, i, b * 4 + w)
                unit(b, 6, 0, b * 4 + 3)
                unit(b, 7, 1, b * 4 + 3, ge=not last)

            gate(0)
            phase_a(0, False)
            with act.Fori(0, NB - 1) as b:
                sample(b, False)
                phase_a(b + 1, True)
            sample(NB - 1, True)
            z_relu(NB - 1, NU - 1, 1, (NB - 1) * 4 + 3)

        @block.vector
        def _(dve):
            v = nc.vector
            set_n = [0]

            def link(ins, s, n):
                ins.then_inc(s, 1)
                dve.wait_ge(s, n)

            def lk(ins):
                set_n[0] += 1
                link(ins, s_dcs, set_n[0])

            v.memset(t[:, :, :], 0.0).then_inc(s_set, 1)
            v.memset(ones9[:, :], 1.0)
            v.memset(ep, 0.0)
            lk(v.memset(skv, 1.0))
            dve.wait_ge(s_in, 16 * N_IN)
            lk(v.tensor_scalar(ang[:, 0:18], ang[:, 0:18], 0.5, None, ALU.mult))
            lk(v.tensor_scalar(ang[:, 18:36], ang[:, 18:36], 0.5, TWO_PI / 4, ALU.mult, ALU.add))
            lk(v.tensor_scalar(angn, ang, 1.0 / TWO_PI, MAGIC, ALU.mult, ALU.add))
            lk(v.tensor_scalar(angn, angn, MAGIC, None, ALU.subtract))
            lk(v.scalar_tensor_tensor(ang, angn, -6.28125, ang, ALU.mult, ALU.add))
            lk(v.scalar_tensor_tensor(ang, angn, 6.28125 - TWO_PI, ang, ALU.mult, ALU.add))
            lk(v.tensor_scalar(ang, ang, 3.1415925, -3.1415925, ALU.min, ALU.max))
            v.tensor_scalar(bsc[:, :], bn[:, 3, :], BN_EPS, None, ALU.add).then_inc(s_set, 1)
            dve.wait_ge(s_scl, 1)
            lk(v.tensor_tensor(bsc[:, :], bn[:, 0, :], bsh[:, :], ALU.mult))
            lk(v.tensor_tensor(bsh[:, :], bn[:, 2, :], bsc[:, :], ALU.mult))
            lk(v.tensor_tensor(bsh[:, :], bn[:, 1, :], bsh[:, :], ALU.subtract))
            lk(v.tensor_copy(skv[0:DV, :], bsc[0:DV, 7:8]))
            lk(v.tensor_scalar(w1n, w1n, bsc[:, 0:1], None, ALU.mult))
            for oc in range(CC):
                lk(v.tensor_scalar(w3n[:, oc * P:(oc + 1) * P], w3n[:, oc * P:(oc + 1) * P], bsc[:, 3 + oc:4 + oc],
                                   None, ALU.mult))
            lk(v.tensor_scalar(wqn, wqn, bsc[0:64, 1:2], None, ALU.mult))
            lk(v.tensor_scalar(wkvn, wkvn, skv, None, ALU.mult))
            v.tensor_copy(tvb, bsh[0:DV, 7:8].broadcast_to([DV, P])).then_inc(s_set, 1)

            dve.wait_ge(s_trig, 1)
            lk(v.tensor_scalar(ang, angn, -1.0, None, ALU.mult))
            sn, cs, ns = angn[:, 0:18], angn[:, 18:36], ang[:, 0:18]
            for m, (bit, on, off) in enumerate(((gits, sn, cs), (gits, cs, ns), (bits, ns, cs), (bits, cs, sn))):
                lo = 0 if m < 2 else NQ
                lk(v.tensor_scalar(nbit[:, :, :].rearrange("p c q -> p (c q)"),
                                   bit.rearrange("p c q -> p (c q)"), -1.0, 1.0, ALU.mult, ALU.add))
                for kc in range(CC):
                    lk(v.tensor_tensor(al[:, m, kc, :], bit[:, kc, :], on[:, lo:lo + NQ], ALU.mult))
                    lk(v.tensor_tensor(nbit[:, kc, :], nbit[:, kc, :], off[:, lo:lo + NQ], ALU.mult))
                    lk(v.tensor_tensor(al[:, m, kc, :], al[:, m, kc, :], nbit[:, kc, :], ALU.add))
            for mat, dest in ((0, m0), (1, g1)):
                for kc in range(CC):
                    a = lambda q: al[:, 2 * mat, kc, q:q + 1]
                    b_ = lambda q: al[:, 2 * mat + 1, kc, q:q + 1]
                    cur = dbl[0]
                    lk(v.tensor_copy(cur[:, 0:1], a(0)))
                    lk(v.tensor_copy(cur[:, 1:2], b_(0)))
                    for q in range(1, NQ):
                        n = 1 << q
                        nxt = dest[:, kc, :] if q == NQ - 1 else dbl[q % 2]
                        if mat == 0:
                            o = nxt[:, 0:2 * n].rearrange("p (m i) -> p m i", i=2)
                            lk(v.tensor_scalar(o[:, :, 0], cur[:, 0:n], a(q), None, ALU.mult))
                            lk(v.tensor_scalar(o[:, :, 1], cur[:, 0:n], b_(q), None, ALU.mult))
                        else:
                            o = nxt[:, 0:2 * n].rearrange("p (m i) -> p m i", i=4)
                            i_ = cur[:, 0:n].rearrange("p (m i) -> p m i", i=2)
                            lk(v.tensor_scalar(o[:, :, 0:4:3], i_, a(q), None, ALU.mult))
                            lk(v.tensor_scalar(o[:, :, 1:3], i_, b_(q), None, ALU.mult))
                        cur = nxt
            v.memset(st[:, 0, 0, 0:1], 0.0).then_inc(s_set, 1)

            v3 = ep.rearrange("p (r c) -> p r c", r=EPR)
            lk(v.tensor_copy(v3[:, 3:3 + R, 4:4 + R], embn.rearrange("p (r c) -> p r c", r=R)))
            split(v, lk, ep, er, ehp)
            pick(v, lk, er, ehp, ep8)
            v8 = ep8.rearrange("p (r c) -> p r c", r=EPR)
            for oy in range(4):
                for ox in range(4):
                    for c in range(3):
                        o = e8[:, (oy * 4 + ox) * 3 + c, :].rearrange("p (d r m) -> p d r m", d=WCD, r=WROWS)
                        r0 = WROWS * c - oy + 3
                        src = bass.AP(v8.tensor, v8.offset + r0 * EPC + 3 - ox,
                                      [list(v8.ap[0]), [4, WCD], [EPC, WROWS], [1, WCM]])
                        v.tensor_copy(o, src)
            dve.wait_ge(s_spe, 2)
            for jc in range(CC):
                v.tensor_copy(ut[:, jc, :], (CO + VO)[jc][:, :]).then_inc(s_co if jc < 2 else s_vev, 1)

            def gcoef(b, final=None):
                n = [0]

                def lg(ins):
                    n[0] += 1
                    link(ins, s_dc, NG * b + n[0])

                def ready(ins, s, k):
                    link(ins, s, k)

                G = lambda i: g[:, i, :]
                mv = g[:, 0:2, :].rearrange("p a b -> p (a b)")
                mean, var = mv[:, 0:8:2], mv[:, 1:8:2]
                dve.wait_ge(s_bs, NU * (b + 1))
                v.memset(G(27), 0.0)
                for oc in range(CC):
                    ins = v.bn_aggr(mv[:, 2 * oc:2 * oc + 2], st[:, oc, :, :].rearrange("p u s -> p (u s)"))
                ready(ins, s_gd, 8 * b + 1)
                dve.wait_ge(s_gp, 8 * b + 1)
                lg(v.tensor_copy(G(27), SM[:, 0:4]))
                lg(v.tensor_tensor(G(2), mean, G(27), ALU.subtract))
                lg(v.tensor_tensor(G(3), G(2), G(2), ALU.mult))
                ready(v.tensor_tensor(G(3), G(3), var, ALU.add), s_gd, 8 * b + 2)
                dve.wait_ge(s_gp, 8 * b + 2)
                v.tensor_scalar(G(4), SM[:, 4:8], GN_EPS0, None, ALU.add).then_inc(s_gv, 1)
                dve.wait_ge(s_gl, 2 * b + 1)
                lg(v.tensor_tensor(G(6), G(2), G(5), ALU.mult))
                ready(v.tensor_tensor(G(7), G(6), G(6), ALU.mult), s_gd, 8 * b + 3)
                dve.wait_ge(s_gp, 8 * b + 3)
                lg(v.tensor_copy(G(8), SM[:, 8:12]))
                ready(v.tensor_tensor(G(9), G(8), G(8), ALU.mult), s_gd, 8 * b + 4)
                dve.wait_ge(s_gp, 8 * b + 4)
                lg(v.reciprocal(g[0:NQ, 10, 0:1], SM[0:NQ, 13:14]))
                ready(v.tensor_tensor(g[0:NQ, 11, 0:1], SM[0:NQ, 12:13], g[0:NQ, 10, 0:1], ALU.mult), s_gd, 8 * b + 5)
                if final:
                    final()
                dve.wait_ge(s_gp, 8 * b + 5)
                v.tensor_tensor(G(12), SM[:, 14:18], fcb_s[:, :], ALU.add).then_inc(s_gx, 1)
                dve.wait_ge(s_ge, b + 1)
                lg(v.tensor_scalar(G(13), G(13), 1.0, None, ALU.add))
                lg(v.reciprocal(G(14), G(13)))
                lg(v.tensor_tensor(G(15), G(14), G(5), ALU.mult))
                lg(v.tensor_scalar(G(16), G(15), 1.0, None, ALU.add))
                lg(v.scalar_tensor_tensor(G(21), G(27), -1.0, G(15), ALU.mult, ALU.mult))
                lg(v.tensor_tensor(G(17), G(14), G(6), ALU.mult))
                ready(v.tensor_tensor(G(17), G(17), mean, ALU.add), s_gd, 8 * b + 6)
                lg(v.tensor_tensor(G(19), G(16), G(16), ALU.mult))
                lg(v.tensor_tensor(G(19), G(19), var, ALU.mult))
                dve.wait_ge(s_gp, 8 * b + 6)
                lg(v.tensor_copy(G(18), SM[:, 18:22]))
                lg(v.tensor_tensor(G(20), G(17), G(18), ALU.subtract))
                lg(v.tensor_tensor(G(20), G(20), G(20), ALU.mult))
                ready(v.tensor_tensor(G(20), G(20), G(19), ALU.add), s_gd, 8 * b + 7)
                dve.wait_ge(s_gp, 8 * b + 7)
                v.tensor_scalar(G(22), SM[:, 22:26], GN_EPS0, None, ALU.add).then_inc(s_gv, 1)
                lg(v.tensor_tensor(G(24), G(21), G(18), ALU.subtract))
                dve.wait_ge(s_gl, 2 * b + 2)
                lg(v.tensor_tensor(G(24), G(24), G(26), ALU.mult))
                lg(v.tensor_tensor(G(23), G(16), G(26), ALU.mult))
                lg(v.tensor_tensor(G(25), G(24), bsh[:, 3:7], ALU.add))
                lg(v.tensor_tensor(G(25), G(25), G(21), ALU.add))
                for oc in range(CC):
                    ins = v.tensor_scalar(w1s[:, oc, :], w1t[:, oc, :], g[:, 23, oc:oc + 1], None, ALU.mult)
                ready(ins, s_gd, 8 * b + 8)
                dve.wait_ge(s_gp, 8 * b + 8)
                v.tensor_tensor(bias1[:, :], SM[:, 26:27], bsh[:, 0:1], ALU.add).then_inc(s_gb, 1)
                assert n[0] == NG, n

            def stats(b, k):
                for oc in range(CC):
                    ins = v.bn_stats(st[:, oc, k, :], xs(b, k, oc))
                ins.then_inc(s_bs, 1)

            def final(b, u, par):
                U = b * NU + u
                for oc in range(CC):
                    dve.wait_ge(s_c3, 4 * U + oc + 1)
                    dve.wait_ge(s_fin, 4 * U + oc + 1)
                    tt = t[:, oc % 2, :]
                    link(v.scalar_tensor_tensor(tt, xs(b, u, oc), coef[:, 0, oc:oc + 1], CO[oc % 2][:, :],
                                                ALU.mult, ALU.add), s_co, 4 * U + oc + 3)
                    v.tensor_scalar(tt, tt, coef[:, 1, oc:oc + 1], coef[:, 2, oc:oc + 1], ALU.add, ALU.max
                                    ).then_inc(s_t, 1)

            def pair(b, a):
                pi = b * PAIRS + a
                for i in range(2):
                    n = 8 * a + 4 * i
                    kv = PB[i][:, 0:192].rearrange("p (n c) -> p n c", c=48)
                    dve.wait_ge(s_kv, 2 * pi + i + 1)
                    v.tensor_tensor(vt[:, bass.ds(n, 4), :], kv[:, :, 0:DV],
                                    bvb[:, :].unsqueeze(1).broadcast_to([P, 4, DV]), ALU.add)
                    mx = kmx[:, bass.ds(n, 4)]
                    link(v.reduce_max(mx, kv[:, :, DV:48], AXX), s_km, 2 * pi + i + 1)
                    v.tensor_tensor(kt[:, bass.ds(n, 4), :], kv[:, :, DV:48],
                                    mx.unsqueeze(2).broadcast_to([P, 4, DK]), ALU.subtract).then_inc(s_kvev, 1)

            def move_coef(b):
                dve.wait_ge(s_fin, 2 + 4 * NU * b)
                for i, k in enumerate((26, 25, 21)):
                    last = v.tensor_copy(coef[:, i, :], g[:, k, :])
                last.then_inc(s_cf, 1)

            def phase_a(b, prev):
                pair(b, 0)
                if prev:
                    final(b - 1, NU - 1, 1)
                move_coef(b)
                with dve.Fori(1, PAIRS) as a:
                    pair(b, a)
                dve.wait_ge(s_ex, PAIRS * (b + 1))
                link(v.reduce_sum(ksum[:, :], kt[:, :, :], AXX), s_sc, 2 * b + 1)
                link(v.reciprocal(ksum[:, :], ksum[:, :]), s_sc, 2 * b + 2)
                v.tensor_tensor(kt[:, :, :], kt[:, :, :], ksum[:, :].unsqueeze(2).broadcast_to([P, 32, DK]),
                                ALU.mult).then_inc(s_kn, 1)

            def content(b):
                n = [0]
                dve.wait_ge(s_cf, b + 1)

                def ll(ins):
                    n[0] += 1
                    link(ins, s_lc, NL * b + n[0])

                dve.wait_ge(s_cl, 2 * b + 1)
                v.tensor_copy(cls[:, :], SM[0:DK, 32:64]).then_inc(s_clc, 1)
                dve.wait_ge(s_cl, 2 * b + 2)
                ll(v.tensor_copy(clf[:, 0, :], SM[:, 64:96]))
                split(v, ll, clf[:, 0, :], clf[:, 1, :], [clh[:, i, :] for i in range(3)])
                pick(v, ll, clf[:, 1, :], [clh[:, i, :] for i in range(3)], cl8[:, :], (s_clc, 1))
                assert n[0] == NL, n

            def sample(b, last):
                content(b)
                final(b, 0, 0)
                if not last:
                    for k in range(2):
                        dve.wait_ge(s_x[k], 16 * (b * 4 + 5))
                        stats(b + 1, k)
                with dve.Fori(1, 3) as w:
                    for i in range(2):
                        if not last:
                            dve.wait_ge(s_x[i], 16 * (b * 4 + 5 + w))
                            for oc in range(CC):
                                ins = v.bn_stats(st[:, oc, bass.ds(2 * w + i, 1), :].rearrange("p u s -> p (u s)"),
                                                 xs(b + 1, 2 * w + i, oc))
                            ins.then_inc(s_bs, 1)
                        final(b, 2 * w + i - 1, 1 - i)
                if not last:
                    for k in (6, 7):
                        dve.wait_ge(s_x[k - 6], 16 * (b * 4 + 8))
                        stats(b + 1, k)
                final(b, 5, 1)
                if last:
                    final(b, 6, 0)
                else:
                    gcoef(b + 1, lambda: final(b, 6, 0))

            for k in range(NU):
                dve.wait_ge(s_x[k % 2], 16 * (k // 2 + 1))
                stats(0, k)
            gcoef(0)
            phase_a(0, False)
            with dve.Fori(0, NB - 1) as b:
                sample(b, False)
                phase_a(b + 1, True)
            sample(NB - 1, True)
            final(NB - 1, NU - 1, 1)

        @block.gpsimd
        def _(pool):
            v = nc.gpsimd

            def link(ins, s, n):
                ins.then_inc(s, 1)
                pool.wait_ge(s, n)

            v.memset(zero_s[:, :], 0.0)
            link(v.memset(half[:, :], -0.5), s_fin, 1)
            pool.wait_ge(s_set, 2)
            v.tensor_tensor(bsh[:, :], bsc[:, :], half[:, :], ALU.pow).then_inc(s_scl, 1)
            v.memset(qf[:, 0:1], 0.0).then_inc(s_fin, 1)

            def root(b, k):
                pool.wait_ge(s_gv, 2 * b + k + 1)
                v.tensor_tensor(g[:, 26 if k else 5, :], g[:, 22 if k else 4, :], half[:, 0:4], ALU.pow
                                ).then_inc(s_gl, 1)

            def q_parts(b, a):
                pi = b * PAIRS + a
                pool.wait_ge(s_qf, pi + 1)
                pool.wait_ge(s_qw, 32 * pi)
                n, zeros = [0], zero_s[:, 0:1].broadcast_to([P, 512])

                def lp(ins):
                    n[0] += 1
                    link(ins, s_pc, 5 * pi + n[0])

                lp(v.tensor_tensor(qp[:, 0, :], qf[:, :], zeros, ALU.add))
                lp(v.tensor_tensor(qf[:, :], qf[:, :], qp[:, 0, :], ALU.subtract))
                lp(v.tensor_tensor(qp[:, 1, :], qf[:, :], zeros, ALU.add))
                lp(v.tensor_tensor(qf[:, :], qf[:, :], qp[:, 1, :], ALU.subtract))
                v.tensor_tensor(qp[:, 2, :], qf[:, :], zeros, ALU.add).then_inc(s_pc, 1)

            def final(b, u, par, cnt):
                U = b * NU + u
                for oc in range(CC):
                    pool.wait_ge(s_t, 4 * U + oc + 1)
                    o = xs(b, u, oc)
                    ins = v.tensor_tensor(o, o, t[:, oc % 2, :], ALU.add)
                    ins.then_inc(s_fin, 1)
                pool.wait_ge(s_fin, 2 + 4 * (U + 1))
                pool.wait_ge(s_st[par], 16 * cnt)
                pool.dma_start(dram_unit(out_v, b, u), xslot(b, u)).then_inc(s_st[par], 16)

            def phase_a(b, prev):
                q_parts(b, 0)
                if prev:
                    final(b - 1, NU - 1, 1, (b - 1) * 4 + 3)
                with pool.Fori(1, PAIRS) as a:
                    q_parts(b, a)

            def sample(b, last):
                final(b, 0, 0, b * 4)
                with pool.Fori(1, 3) as w:
                    final(b, 2 * w - 1, 1, b * 4 + w - 1)
                    final(b, 2 * w, 0, b * 4 + w)
                final(b, 5, 1, b * 4 + 2)
                if not last:
                    root(b + 1, 0)
                final(b, 6, 0, b * 4 + 3)
                if not last:
                    root(b + 1, 1)

            root(0, 0)
            root(0, 1)
            phase_a(0, False)
            with pool.Fori(0, NB - 1) as b:
                sample(b, False)
                phase_a(b + 1, True)
            sample(NB - 1, True)
            final(NB - 1, NU - 1, 1, (NB - 1) * 4 + 3)
    return nc


NG = 22
NL = 8


def split(v, link, f, r, parts):
    link(v.tensor_copy(parts[0], f))
    link(v.tensor_tensor(f, f, parts[0], ALU.subtract))
    link(v.tensor_copy(parts[1], f))
    link(v.tensor_tensor(f, f, parts[1], ALU.subtract))
    link(v.tensor_copy(parts[2], f))


def kernel(**inputs):
    import concourse.bacc as bacc
    from concourse.bass_utils import run_bass_kernel_spmd

    a = {k: np.asarray(w) for k, w in inputs.items()}
    l1 = lambda n: a["L1_conv_" + n]
    kh = lambda w: w.reshape(HD, DK, -1).swapaxes(0, 1).reshape(w.shape)
    vh = lambda w: w.reshape(HD, DV, -1).swapaxes(0, 1).reshape(w.shape)
    rows = lambda n: np.stack([l1("bn1_" + n), np.tile(kh(l1("bnq_" + n)), 2), vh(l1("bn2_" + n)),
                               *l1("bn3_" + n).reshape(CC, P), np.tile(l1("bnv_" + n), 4)], axis=1)
    k = np.arange(C).reshape(CC, P).T
    bit = lambda i: ((i[:, :, None] >> np.arange(NQ - 1, -1, -1)) & 1).astype(np.float32)
    rowsq = np.arange(P)
    emb_part = np.array([0, 1, 2, 0, 1, 2, 0, 1])[rowsq // DK]
    consts = {
        "kbit": bit(k), "gbit": bit(k ^ (k >> 1)), "sign": 1 - 2 * bit(k),
        "ident": np.eye(P, dtype=np.float32),
        "gavg": (rowsq[:, None] // GRP == rowsq // GRP).astype(np.float32) / GRP,
        "mask": (emb_part[:, None] == np.arange(3)).astype(np.float32),
        "rep": (rowsq % DK == np.arange(DK)[:, None]).astype(np.float32),
    }
    arrays = {
        "x": a["x"].reshape(NB, C, HW),
        "bnp": np.stack([rows("g"), rows("b"), rows("m"), rows("v")], axis=1),
        "w1": l1("conv1_w"), "w3": vh(l1("conv3_w").T).T, "wq": kh(l1("q_w")),
        "wkv": np.concatenate([l1("v_w"), l1("k_w")]),
        "emb": np.tile(l1("emb").reshape(DK, R * R), (P // DK, 1)),
        "qpar": np.broadcast_to(a["L0_conv_q_params"].reshape(1, 2 * NQ), (P, 2 * NQ)),
        "fcw": a["L0_conv_fc_w"].T, "fcb": a["L0_conv_fc_b"].reshape(CC, P).T,
    } | consts
    arrays = {n: np.ascontiguousarray(w) for n, w in arrays.items()}
    nc = bacc.Bacc("TRN2", target_bir_lowering=False, num_devices=1)
    args = {n: nc.dram_tensor("in_" + n, w.shape, mybir.dt.from_np(w.dtype), kind="ExternalInput").ap()
            for n, w in arrays.items()}
    out = nc.dram_tensor("out", (NB, C, HW), F32, kind="ExternalOutput").ap()
    build(nc, **args, out=out)
    r = run_bass_kernel_spmd(nc, [{"in_" + n: w for n, w in arrays.items()}], core_ids=[0])
    return r.results[0]["out"].reshape(NB, C, 64, 64)
```

```python
from contextlib import ExitStack

import concourse.bass as bass
import concourse.mybir as mybir
import numpy as np

F32 = mybir.dt.float32
BF16 = mybir.dt.bfloat16
ALU = mybir.AluOpType
ACT = mybir.ActivationFunctionType
AXX = mybir.AxisListType.X

P = 128
NB, C, HW = 32, 512, 4096
CC = C // P
GRP = 16
NU, UN = 8, 512
PAIRS = NU // 2
SLOTS = 12
SLOT = CC * UN
WD = 128
HD, DK, DV, R = 4, 16, 32, 15
NQ = 9
WROWS, WCM, WCD = 6, 4, 5
WP = WROWS * WCM * WCD
VROWS, NXB = 78, 16
VROW = WCM * NXB * DV
EPR, EPC = 21, 24
NP = 12
GN_EPS0 = 1e-5
BN_EPS = 1e-5
QPART = DK * HD * UN
TWO_PI = 6.283185307179586
MAGIC = 12582912.0


def build(nc, x, bnp, w1, w3, wq, wkv, emb, qpar, fcw, fcb, kbit, gbit, sign, ident, gavg, mask, rep, out):
    ctx = ExitStack()
    with ctx:
        def sb(name, shape, dt=F32):
            return ctx.enter_context(nc.sbuf_tensor(name, shape, dt))

        def pb(name):
            return ctx.enter_context(nc.psum_tensor(name, [P, 512], F32))

        def sem(name):
            return ctx.enter_context(nc.semaphore(name))

        vpad = nc.dram_tensor("vpad", [VROWS * VROW], F32, kind="Internal").ap()
        qparts_d = nc.dram_tensor("qparts_d", [NU * 3 * QPART], BF16, kind="Internal").ap()

        zmove = nc.dram_tensor("zmove", [2 * P * 512], F32, kind="Internal").ap()

        xr = sb("xr", [P, SLOTS * SLOT])
        pw = sb("pw", [P, 2, 32, 64])
        win = sb("win", [P, 2, 6 * 512])
        e8 = sb("e8", [P, 48, WP], BF16)
        ut = sb("ut", [P, CC, C])
        h1 = sb("h1", [P, 2, UN])
        qf = sb("qf", [P, UN])
        qp = sb("qp", [P, 3, UN], BF16)
        q8 = sb("q8", [P, 2, HD, UN], BF16)
        z1 = sb("z1", [P, 2, HD, P])
        z = sb("z", [P, 2, UN])
        t = sb("t", [P, 2, UN])
        w1t = sb("w1t", [P, CC, P])
        w1s = sb("w1s", [P, CC, P])
        w3t = sb("w3t", [P, C])
        wqt = sb("wqt", [P, HD * DK])
        wkvt = sb("wkvt", [P, DV + DK])
        bvb = sb("bvb", [P, DV])
        kt = sb("kt", [P, 32, DK])
        kmx = sb("kmx", [P, 32])
        ksum = sb("ksum", [P, 32])
        vt = sb("vt", [P, 32, DV])
        cls = sb("cls", [DK, DV])
        clf = sb("clf", [P, 3, DV])
        clh = sb("clh", [P, 3, DV], BF16)
        cl8 = sb("cl8", [P, DV], BF16)
        st = sb("st", [P, CC, NU, 6])
        g = sb("g", [P, 30, CC])
        coef = sb("coef", [P, 3, CC])
        bias1 = sb("bias1", [P, 1])
        bn = sb("bn", [P, 4, 8])
        bsc = sb("bsc", [P, 8])
        bsh = sb("bsh", [P, 8])
        half = sb("half", [P, 8])
        zero_s = sb("zero_s", [P, 1])
        fcw_s = sb("fcw_s", [NQ, C])
        fcb_s = sb("fcb_s", [P, CC])
        sign_s = sb("sign_s", [P, CC, NQ])
        id_s = sb("id_s", [P, P])
        gavg_s = sb("gavg_s", [P, P])
        mask_s = sb("mask_s", [P, 3])
        rep_s = sb("rep_s", [DK, P])
        ones9 = sb("ones9", [P, NQ])

        pwf = pw[:, :, :, :].rearrange("p a b c -> p (a b c)")
        winf = win[:, :, :].rearrange("p a b -> p (a b)")
        m0 = pwf[:, 0:2048].rearrange("p (c j) -> p c j", c=CC)
        g1 = pwf[:, 2048:4096].rearrange("p (c i) -> p c i", c=CC)
        w1n, w3n = winf[:, 0:512], winf[:, 512:1024]
        wqn, wkvn = winf[0:64, 1024:1152], winf[0:48, 1152:1280]
        ep = winf[:, 1280:1280 + EPR * EPC]
        er = winf[:, 1792:1792 + EPR * EPC]
        embn = winf[:, 2304:2304 + R * R]
        tvb = winf[0:DV, 2560:2560 + P]
        skv = winf[0:48, 2688:2689]
        ang = winf[:, 2700:2736]
        angn = winf[:, 2740:2776]
        bits = winf[:, 2780:2780 + 36].rearrange("p (c q) -> p c q", c=CC)
        gits = winf[:, 2820:2820 + 36].rearrange("p (c q) -> p c q", c=CC)
        al = winf[:, 2860:2860 + 4 * 36].rearrange("p (m c q) -> p m c q", m=4, c=CC)
        nbit = winf[:, 3004:3004 + 36].rearrange("p (c q) -> p c q", c=CC)
        dbl = [h1[:, 0, :], h1[:, 1, :]]
        eh = q8[:, 0, :, :].rearrange("p a b -> p (a b)")
        ehp = [eh[:, i * 512:i * 512 + EPR * EPC] for i in range(3)]
        ep8 = eh[:, 1536:1536 + EPR * EPC]

        PB = [pb(f"PB{i}") for i in range(3)]
        SM = pb("SM")
        VO = [pb(f"VO{i}") for i in range(2)]
        CO = [pb(f"CO{i}") for i in range(2)]

        s_in = sem("s_in")
        s_zero = sem("s_zero")
        s_wz = sem("s_wz")
        s_set = sem("s_set")
        s_scl = sem("s_scl")
        s_trig = sem("s_trig")
        s_spe = sem("s_spe")
        s_x = [sem(f"s_x{i}") for i in range(2)]
        s_st = [sem(f"s_st{i}") for i in range(2)]
        s_bs = sem("s_bs")
        s_gd = sem("s_gd")
        s_gv = sem("s_gv")
        s_gx = sem("s_gx")
        s_gb = sem("s_gb")
        s_gp = sem("s_gp")
        s_gl = sem("s_gl")
        s_ge = sem("s_ge")
        s_dcs = sem("s_dcs")
        s_dc = sem("s_dc")
        s_km = sem("s_km")
        s_conv = sem("s_conv")
        s_h1 = sem("s_h1")
        s_kv = sem("s_kv")
        s_q = sem("s_q")
        s_qf = sem("s_qf")
        s_pc = sem("s_pc")
        s_qw = sem("s_qw")
        s_kvev = sem("s_kvev")
        s_ex = sem("s_ex")
        s_vw = sem("s_vw")
        s_sc = sem("s_sc")
        s_lc = sem("s_lc")
        s_kn = sem("s_kn")
        s_cl = sem("s_cl")
        s_clc = sem("s_clc")
        s_q8 = [sem(f"s_q8{i}") for i in range(2)]
        s_win = [sem(f"s_win{i}") for i in range(2)]
        s_p = sem("s_p")
        s_pev = sem("s_pev")
        s_vst = sem("s_vst")
        s_vo = sem("s_vo")
        s_vev = sem("s_vev")
        s_zd = [sem(f"s_zd{i}") for i in range(2)]
        s_z = [sem(f"s_z{i}") for i in range(2)]
        s_zr = sem("s_zr")
        s_c3 = sem("s_c3")
        s_co = sem("s_co")
        s_t = sem("s_t")
        s_fin = sem("s_fin")
        s_cf = sem("s_cf")

        N_IN = 11
        block = ctx.enter_context(nc.Block())

        def wait_each(eng, *waits):
            values = [n if isinstance(n, int) else eng.snap(eng.to_reg(n)) for _, n in waits]
            for (s, _), n in zip(waits, values):
                eng.wait_ge(s, n)

        def pick(v, link, f, parts, out, last=None):
            link(v.tensor_scalar(f, parts[0], mask_s[:, 0:1], None, ALU.mult))
            link(v.scalar_tensor_tensor(f, parts[1], mask_s[:, 1:2], f, ALU.mult, ALU.add))
            ins = v.scalar_tensor_tensor(out, parts[2], mask_s[:, 2:3], f, ALU.mult, ALU.add)
            if last:
                ins.then_inc(*last)
            else:
                link(ins)

        def xs(b, u, oc):
            return xr[:, bass.ds(((b * NU + u) % SLOTS) * SLOT + oc * UN, UN)]

        def xslot(b, u):
            return xr[:, bass.ds(((b * NU + u) % SLOTS) * SLOT, SLOT)].rearrange("p (c n) -> p c n", c=CC)

        x_v = x.rearrange("b (c p) n -> b p c n", p=P)
        out_v = out.rearrange("b (c p) n -> b p c n", p=P)

        def dram_unit(v, b, u):
            return v[bass.ds(b, 1), :, :, bass.ds(u * UN, UN)].rearrange("b p c n -> (b p) c n")

        @block.sync
        def _(sp):
            for dst, src in ((bn[:, :, :], bnp), (w1n, w1), (w3n.rearrange("p (c v) -> p c v", c=CC),
                             w3.rearrange("(c p) v -> p c v", p=P)), (wqn, wq), (wkvn, wkv), (embn, emb),
                             (ang[:, 0:18], qpar), (ang[:, 18:36], qpar), (bits, kbit), (gits, gbit),
                             (id_s[:, :], ident)):
                sp.dma_start(dst, src).then_inc(s_in, 16)
            for s, dst, src in ((s_z[0], fcw_s[:, :], fcw), (s_z[1], sign_s[:, :, :], sign)):
                sp.dma_start(dst, src).then_inc(s, 16)

            def load_x(b, k, par):
                sp.dma_start(xslot(b, k), dram_unit(x_v, b, k)).then_inc(s_x[par], 16)

            for k in range(NU):
                if k >= 2:
                    sp.wait_ge(s_x[k % 2], 16 * (k // 2))
                load_x(0, k, k % 2)
            sp.wait_ge(s_set, 1)
            flat = t[:, :, :].rearrange("p a b -> p (a b)")
            body = VROWS * VROW // P
            vz = vpad.rearrange("(p n) -> p n", p=P)
            for o in range(0, body, 1024):
                n = min(1024, body - o)
                sp.dma_start(vz[:, o:o + n], flat[:, 0:n]).then_inc(s_zero, 16)
            sp.wait_ge(s_zero, 16 * (-(-body // 1024)))

            def z_load(b, u, par, cnt):
                sp.wait_ge(s_zd[par], 16 * (cnt + 1))
                src = bass.AP(zmove.tensor, par * (P * 512), [[P, P], [DV * 512, 4], [1, P]])
                sp.dma_start(z[:, par, :].rearrange("p (j n) -> p j n", j=4), src).then_inc(s_z[par], 16)

            def q8_load(u, par):
                for lo, n, part in ((0, 3, 0), (48, 3, 1), (96, 2, 2)):
                    src = bass.AP(qparts_d.tensor, u * (3 * QPART) + part * QPART, [[0, n], [HD * UN, DK], [1, HD * UN]])
                    sp.dma_start(q8[lo:lo + DK * n, par, :, :].rearrange("p h n -> p (h n)"), src
                                 ).then_inc(s_q8[par], 16)

            def win_load(u, par):
                dst = win[:, par, :].rearrange("p (c y n) -> p c y n", c=3, y=2)
                for yb in range(2):
                    for cd in range(WCD):
                        lo, hi = max(0, 2 - cd), min(NXB, NXB + 2 - cd)
                        src = bass.AP(vpad.tensor, u * (8 * VROW) + (4 * yb * VROW + (lo + cd - 2) * DV),
                                      [[NXB * DV, WROWS * WCM], [WROWS * VROW, 3], [1, (hi - lo) * DV]])
                        sp.dma_start(dst[cd * 24:cd * 24 + 24, :, yb, lo * DV:hi * DV], src).then_inc(s_win[par], 16)

            def v_store(a):
                dst = bass.AP(vpad.tensor, a * (16 * VROW) + 7 * VROW, [[DV, P], [2 * VROW, 8], [1, DV]])
                sp.dma_start(dst, vt[:, bass.ds(a * 8, 8), :]).then_inc(s_vw, 16)

            def q_store(a):
                for i in range(2):
                    dst = bass.AP(qparts_d.tensor, a * (6 * QPART) + i * 3 * QPART, [[UN, HD * DK], [QPART, 3], [1, UN]])
                    sp.dma_start(dst, qp[64 * i:64 * i + 64, :, :]).then_inc(s_qw, 16)

            def pair_stores(b, a):
                pi = b * PAIRS + a
                wait_each(sp, (s_vw, 16 * pi), (s_kvev, 2 * (pi + 1)))
                v_store(a)
                wait_each(sp, (s_qw, 32 * pi), (s_pc, 5 * (pi + 1)))
                q_store(a)

            def stored(b, a):
                wait_each(sp, (s_vw, 16 * (b * PAIRS + a + 1)), (s_qw, 32 * (b * PAIRS + a + 1)))

            def phase_a(b, prev):
                if prev:
                    sp.wait_ge(s_vev, 2 + b * NU)
                    z_load(b - 1, NU - 1, 1, (b - 1) * 4 + 3)
                pair_stores(b, 0)
                stored(b, 0)
                q8_load(0, 0)
                q8_load(1, 1)
                win_load(0, 0)
                pair_stores(b, 1)
                stored(b, 1)
                win_load(1, 1)
                with sp.Fori(2, PAIRS) as a:
                    pair_stores(b, a)

            def load_next(b, h, par):
                wait_each(sp, (s_x[par], 16 * (b * 4 + h + 5)), (s_st[par], 16 * (b * 4 + h + 2)))
                load_x(b + 1, 2 * h + 2 + par, par)

            def unit(b, u, par, cnt, load, ahead=True, early=False):
                sp.wait_ge(s_vev, 2 + b * NU + u)
                if ahead:
                    q8_load(u + 1, 1 - par)
                    if early:
                        load()
                    win_load(u + 1, 1 - par)
                z_load(b, u - 1, 1 - par, cnt - (1 - par))
                if load and not early:
                    load()

            def sample(b, last):
                n = 16 * PAIRS * (b + 1)
                if not last:
                    wait_each(sp, (s_st[0], 64 * b + 16), (s_st[1], 64 * b + 16), (s_x[0], n), (s_x[1], n))
                    for k in range(2):
                        load_x(b + 1, k, k)
                wait_each(sp, (s_vw, n), (s_qw, 2 * n))
                unit(b, 1, 1, b * 4, None if last else (lambda: load_next(b, 0, 0)))
                with sp.Fori(1, 3) as w:
                    unit(b, 2 * w, 0, b * 4 + w, None if last else (lambda: load_next(b, w - 1, 1)))
                    unit(b, 2 * w + 1, 1, b * 4 + w, None if last else (lambda: load_next(b, w, 0)))
                unit(b, 6, 0, b * 4 + 3, None if last else (lambda: load_next(b, 2, 1)), early=not last)
                unit(b, 7, 1, b * 4 + 3, None, ahead=False)

            sp.wait_ge(s_wz, 1)
            phase_a(0, False)
            with sp.Fori(0, NB - 1) as b:
                sample(b, False)
                phase_a(b + 1, True)
            sample(NB - 1, True)
            z_load(NB - 1, NU - 1, 1, (NB - 1) * 4 + 3)
            sp.wait_ge(s_st[0], 16 * (NB * 4 + 2))
            sp.wait_ge(s_st[1], 16 * (NB * 4 + 2))

        @block.tensor
        def _(pe):
            mm = nc.tensor.matmul
            pe.wait_ge(s_set, 3)
            for oc in range(CC):
                nc.tensor.transpose(PB[0][:, oc * P:(oc + 1) * P], w1n[:, oc * P:(oc + 1) * P], id_s[:, :])
            for oc in range(CC):
                nc.tensor.transpose(PB[1][:, oc * P:(oc + 1) * P], w3n[:, oc * P:(oc + 1) * P], id_s[:, :])
            nc.tensor.transpose(PB[2][:, 0:64], wqn, id_s[0:64, 0:64])
            nc.tensor.transpose(PB[2][:, 64:112], wkvn, id_s[0:48, 0:48])
            mm(PB[2][:, 128:160], tvb, id_s[0:DV, 0:DV], start=True, stop=True).then_inc(s_spe, 1)
            pe.wait_ge(s_set, 4)
            for jc in range(CC):
                o = (CO + VO)[jc]
                for kc in range(CC):
                    last = mm(o[:, :], m0[:, kc, jc * P:(jc + 1) * P], g1[:, kc, :], start=kc == 0, stop=kc == CC - 1)
                    if jc == CC - 1 and kc in (1, 2):
                        last.then_inc(s_vst, 1)
            last.then_inc(s_spe, 1)

            def gstep(b, n):
                pe.wait_ge(s_gd, 8 * b + n)
                if n in (1, 2, 6, 7):
                    col, src = {1: (0, 0), 2: (4, 3), 6: (18, 17), 7: (22, 20)}[n]
                    rhs = mean_ap if n == 1 else g[:, src, :]
                    last = mm(SM[:, col:col + 4], gavg_s[:, :], rhs, start=True, stop=True)
                elif n == 3:
                    for ic in range(CC):
                        for jc in range(CC):
                            last = mm(SM[:, 8 + ic:9 + ic], ut[:, jc, ic * P:(ic + 1) * P], g[:, 6, jc:jc + 1],
                                      start=jc == 0, stop=jc == CC - 1)
                elif n == 4:
                    for jc in range(CC):
                        mm(SM[0:NQ, 12:13], sign_s[:, jc, :], g[:, 9, jc:jc + 1], start=jc == 0, stop=jc == CC - 1)
                    for jc in range(CC):
                        last = mm(SM[0:NQ, 13:14], ones9[:, :], g[:, 7, jc:jc + 1], start=jc == 0, stop=jc == CC - 1)
                elif n == 5:
                    for oc in range(CC):
                        last = mm(SM[:, 14 + oc:15 + oc], fcw_s[:, oc * P:(oc + 1) * P], g[0:NQ, 11, 0:1],
                                  start=True, stop=True)
                else:
                    for oc in range(CC):
                        last = mm(SM[:, 26:27], w1t[:, oc, :], g[:, 24, oc:oc + 1], start=oc == 0, stop=oc == CC - 1)
                last.then_inc(s_gp, 1)

            def conv3(b, u, par, oc):
                U = b * NU + u
                pe.wait_ge(s_zr, U + 1)
                pe.wait_ge(s_co, 4 * U + oc + 1)
                mm(CO[oc % 2][:, :], w3t[:, oc * P:(oc + 1) * P],
                   z[:, par, :].rearrange("p (j y c) -> p y j c", j=4, y=8), start=True, stop=True
                   ).then_inc(s_c3, 1)

            def pair(b, a, co=None):
                pi = b * PAIRS + a
                for i in range(2):
                    if co is not None:
                        pe.wait_ge(s_co, co + i + 1)
                    for k in range(CC):
                        last = mm(CO[i][:, :], w1s[:, k, :], xs(b, 2 * a + i, k), start=k == 0, stop=k == CC - 1)
                    last.then_inc(s_conv, 1)

                def keys_values(i):
                    pe.wait_ge(s_h1, 2 * pi + i + 1)
                    pe.wait_ge(s_kvev, 2 * pi)
                    for n in range(4):
                        last = mm(PB[i][:, n * 48:(n + 1) * 48], h1[:, i, n * P:(n + 1) * P], wkvt[:, :],
                                  start=True, stop=True)
                    last.then_inc(s_kv, 1)

                keys_values(0)
                pe.wait_ge(s_h1, 2 * pi + 2)
                pe.wait_ge(s_qf, pi)
                mm(VO[0][0:64, :], wqt[:, :], h1[:, 0, :], start=True, stop=True)
                mm(VO[0][64:128, :], wqt[:, :], h1[:, 1, :], start=True, stop=True).then_inc(s_q, 1)
                keys_values(1)

            def phase_a(b, prev):
                pe.wait_ge(s_gd, 8 * b + 8)
                if not prev:
                    pair(b, 0)
                    with pe.Fori(1, PAIRS) as a:
                        pair(b, a)
                else:
                    for a in range(PAIRS):
                        pair(b, a, 2 + 4 * (b * NU - 2) + 2 * a)
                        if a < 3:
                            for oc in LATE[a][1:]:
                                conv3(b - 1, LATE[a][0], LATE[a][0] % 2, oc)

            def p_bank(b, u, par, c, oy):
                f = 4 * c + oy
                pe.wait_ge(s_pev, NP * (b * NU + u) + f + 1)
                qv = q8[:, par, :, :].rearrange("p h (y r m d) -> p h y r m d", y=2, r=4, m=4)
                for ox in range(4):
                    last = mm(PB[f % 3][0:WP, ox * P:(ox + 1) * P], e8[:, (oy * 4 + ox) * 3 + c, :],
                              qv[:, :, :, oy, ox, :], start=True, stop=True)
                last.then_inc(s_p, 1)

            def v_quarter(b, u, par, c, k):
                U, yb = b * NU + u, k // 2
                if k == 0:
                    pe.wait_ge(s_pev, 3 + NP * U + 4 * c + 4)
                for xl in (2 * (k % 2), 2 * (k % 2) + 1):
                    for j in range(4):
                        xb = 4 * j + xl
                        o = VO[par][32 * j:32 * j + 32, :].rearrange("p (h y r c) -> p h y r c", h=HD, y=2, r=4)
                        last = mm(o[:, :, yb, :, 4 * xl:4 * xl + 4],
                                  win[0:WP, par, ((c * 2 + yb) * 16 + xb) * DV:((c * 2 + yb) * 16 + xb + 1) * DV],
                                  pw[0:WP, (par * 3 + c) % 2, yb * 16 + xb, :],
                                  start=c == 0 and yb == 0 and xl == 0, stop=False, skip_group_check=True)
                if k == 3:
                    last.then_inc(s_vst, 1)

            def content(b, u, par):
                for h in range(HD):
                    for j in range(4):
                        qv = q8[:, par, h, :].rearrange("p (y m d) -> p y d m", y=8, m=4)
                        last = mm(VO[par][32 * j:32 * j + 32, h * P:(h + 1) * P], cl8[:, :],
                                  qv[:, :, 4 * j:4 * j + 4, :], start=False, stop=True, skip_group_check=True)
                last.then_inc(s_vo, 1)

            def unit(b, w, par, between=None, spread=None, steps=""):
                u, cnt = 2 * w + par, b * 4 + w
                U = b * NU + u
                step = lambda k: gstep(b + 1, k) if str(k) in steps else None
                pe.wait_ge(s_q8[par], 48 * (cnt + 1))
                for k in range(4):
                    p_bank(b, u, par, 0, k)
                    if between:
                        between(k)
                step(3)
                p_bank(b, u, par, 1, 0)
                p_bank(b, u, par, 1, 1)
                pe.wait_ge(s_win[par], 160 * (cnt + 1))
                pe.wait_ge(s_vev, U + 1)
                v_quarter(b, u, par, 0, 0)
                p_bank(b, u, par, 1, 2)
                v_quarter(b, u, par, 0, 1)
                p_bank(b, u, par, 1, 3)
                v_quarter(b, u, par, 0, 2)
                step(4)
                v_quarter(b, u, par, 0, 3)
                if spread:
                    spread()
                for k in range(4):
                    if k == 0:
                        p_bank(b, u, par, 2, 0)
                    if k < 3:
                        p_bank(b, u, par, 2, k + 1)
                    v_quarter(b, u, par, 1, k)
                    if k == 1:
                        step(5)
                v_quarter(b, u, par, 2, 0)
                v_quarter(b, u, par, 2, 1)
                step(6)
                v_quarter(b, u, par, 2, 2)
                v_quarter(b, u, par, 2, 3)
                if spread:
                    pe.wait_ge(s_clc, 2 * b + 2)
                content(b, u, par)
                for k in (1, 2, 7):
                    step(k)

            def sample(b, last):
                pe.wait_ge(s_kvev, NU * (b + 1))
                pe.wait_ge(s_qf, PAIRS * (b + 1))

                def lambdas(k):
                    if k == 3:
                        pe.wait_ge(s_kn, b + 1)
                        for n in range(32):
                            last = mm(SM[0:DK, 32:64], kt[:, n, :], vt[:, n, :], start=n == 0, stop=n == 31)
                        last.then_inc(s_cl, 1)

                def spread():
                    pe.wait_ge(s_clc, 2 * b + 1)
                    mm(SM[:, 64:96], rep_s[:, :], cls[:, :], start=True, stop=True).then_inc(s_cl, 1)

                unit(b, 0, 0, between=lambdas, spread=spread)
                unit(b, 0, 1)
                with pe.Fori(1, 3) as w:
                    unit(b, w, 0, between=lambda oc: conv3(b, 2 * w - 2, 0, oc))
                    unit(b, w, 1, between=lambda oc: conv3(b, 2 * w - 1, 1, oc))
                unit(b, 3, 0, between=lambda oc: conv3(b, 4, 0, oc), steps="" if last else "12")
                unit(b, 3, 1, between=lambda oc: conv3(b, 5, 1, oc), steps="" if last else "34567")
                conv3(b, 6, 0, 0)
                conv3(b, 6, 0, 1)
                if not last:
                    gstep(b + 1, 8)
                    return
                conv3(b, 6, 0, 2)
                conv3(b, 6, 0, 3)

            mean_ap = g[:, 0:2, :].rearrange("p a b -> p (a b)")[:, 0:8:2]
            for k in range(1, 9):
                gstep(0, k)
            phase_a(0, False)
            with pe.Fori(0, NB - 1) as b:
                sample(b, False)
                phase_a(b + 1, True)
            sample(NB - 1, True)
            for oc in range(CC):
                conv3(NB - 1, NU - 1, 1, oc)

        @block.scalar
        def _(act):
            act.wait_ge(s_set, 2)
            nc.scalar.activation(angn, ang, ACT.Sin).then_inc(s_trig, 1)

            act.wait_ge(s_spe, 1)
            for i, (dst, src) in enumerate(((w1t[:, :, :].rearrange("p c o -> p (c o)"), PB[0][:, :]),
                                            (w3t[:, :], PB[1][:, :]), (wqt[:, :], PB[2][:, 0:64]),
                                            (wkvt[:, :], PB[2][:, 64:112]), (bvb[:, :], PB[2][:, 128:160]))):
                ins = nc.scalar.activation(dst, src, ACT.Copy)
                if i in (0, 1, 4):
                    ins.then_inc(s_pev, 1)

            def z_relu(b, u, par, cnt):
                act.wait_ge(s_z[par], 16 * (cnt + 2))
                nc.scalar.activation(z[:, par, :], z[:, par, :], ACT.Relu, bias=bsh[:, 2:3], scale=bsc[:, 2:3]
                                     ).then_inc(s_zr, 1)

            def scale(b, u):
                for oc in range(CC):
                    nc.scalar.activation(xs(b, u, oc), xs(b, u, oc), ACT.Copy, scale=g[:, 16, oc:oc + 1])

            def pair(b, a, prev, last=False):
                pi = b * PAIRS + a
                for i in range(2):
                    act.wait_ge(s_conv, 2 * pi + i + 1)
                    nc.scalar.activation(h1[:, i, :].rearrange("p (y m d) -> p y d m", y=8, m=4),
                                         CO[i][:, :].rearrange("p (y d m) -> p y d m", y=8, m=4),
                                         ACT.Relu, bias=bias1[:, :]).then_inc(s_h1, 1)
                act.wait_ge(s_q, pi + 1)
                act.wait_ge(s_pc, 5 * pi)
                nc.scalar.activation(qf[:, :], VO[0][:, :], ACT.Identity, bias=bsh[:, 1:2]).then_inc(s_qf, 1)
                if prev:
                    z_relu(b - 1, NU - 1, 1, (b - 1) * 4 + 3)
                if not last:
                    scale(b, 2 * a)
                    scale(b, 2 * a + 1)
                act.wait_ge(s_kvev, 2 * pi + 2)
                kp = kt[:, bass.ds(a * 8, 8), :]
                nc.scalar.activation(kp, kp, ACT.Exp).then_inc(s_ex, 1)

            def phase_a(b, prev):
                act.wait_ge(s_gb, b + 1)
                pair(b, 0, prev)
                with act.Fori(1, PAIRS - 1) as a:
                    pair(b, a, False)
                pair(b, PAIRS - 1, False, last=True)

            def p_copy(b, u, par, c):
                U = b * NU + u
                act.wait_ge(s_vst, 3 * U + c + 1)
                for oy in range(4):
                    f = 4 * c + oy
                    act.wait_ge(s_p, NP * U + f + 1)
                    dst = pw[0:WP, (par * 3 + c) % 2, :, :].rearrange("p k (h r o) -> p r o h k", h=HD, r=4)
                    nc.scalar.activation(dst[:, oy], PB[f % 3][0:WP, :].rearrange("p (o h k) -> p o h k", o=4, h=HD),
                                         ACT.Copy).then_inc(s_pev, 1)

            def unit(b, u, par, cnt, zr=True, ge=False, sc=None):
                U = b * NU + u
                p_copy(b, u, par, 0)
                p_copy(b, u, par, 1)
                p_copy(b, u, par, 2)
                if ge:
                    gate(b + 1)
                if sc:
                    scale(b, sc)
                if zr:
                    z_relu(b, u - 1, 1 - par, cnt - (1 - par))
                act.wait_ge(s_vo, U + 1)
                act.wait_ge(s_z[par], 16 * (cnt + 1))
                nc.scalar.activation(z1[:, par, :, :].rearrange("p h n -> p (h n)"), VO[par][:, :], ACT.Copy
                                     ).then_inc(s_vev, 1)
                act.wait_ge(s_vev, U + 3)
                act.dma_start(bass.AP(zmove.tensor, par * (P * 512), [[512, P], [1, 512]]),
                              z1[:, par, :, :].rearrange("p h n -> p (h n)")).then_inc(s_zd[par], 16)

            def gate(b):
                act.wait_ge(s_gx, b + 1)
                nc.scalar.activation(g[:, 13, :], g[:, 12, :], ACT.Exp, scale=-1.0).then_inc(s_ge, 1)

            def sample(b, last):
                unit(b, 0, 0, b * 4, zr=False, sc=NU - 2)
                unit(b, 1, 1, b * 4, sc=NU - 1)
                with act.Fori(1, 3) as w:
                    for i in range(2):
                        unit(b, 2 * w + i, i, b * 4 + w)
                unit(b, 6, 0, b * 4 + 3)
                unit(b, 7, 1, b * 4 + 3, ge=not last)

            gate(0)
            phase_a(0, False)
            with act.Fori(0, NB - 1) as b:
                sample(b, False)
                phase_a(b + 1, True)
            sample(NB - 1, True)
            z_relu(NB - 1, NU - 1, 1, (NB - 1) * 4 + 3)

        @block.vector
        def _(dve):
            v = nc.vector
            set_n = [0]

            def link(ins, s, n):
                ins.then_inc(s, 1)
                dve.wait_ge(s, n)

            def lk(ins):
                set_n[0] += 1
                link(ins, s_dcs, set_n[0])

            v.memset(t[:, :, :], 0.0).then_inc(s_set, 1)
            v.memset(ones9[:, :], 1.0)
            v.memset(ep, 0.0)
            lk(v.memset(skv, 1.0))
            dve.wait_ge(s_in, 16 * N_IN)
            for s, n in zip((*s_st, *s_z), (32, 32, 16, 16)):
                dve.wait_ge(s, n)
            lk(v.tensor_scalar(ang[:, 0:18], ang[:, 0:18], 0.5, None, ALU.mult))
            lk(v.tensor_scalar(ang[:, 18:36], ang[:, 18:36], 0.5, TWO_PI / 4, ALU.mult, ALU.add))
            lk(v.tensor_scalar(angn, ang, 1.0 / TWO_PI, MAGIC, ALU.mult, ALU.add))
            lk(v.tensor_scalar(angn, angn, MAGIC, None, ALU.subtract))
            lk(v.scalar_tensor_tensor(ang, angn, -6.28125, ang, ALU.mult, ALU.add))
            lk(v.scalar_tensor_tensor(ang, angn, 6.28125 - TWO_PI, ang, ALU.mult, ALU.add))
            lk(v.tensor_scalar(ang, ang, 3.1415925, -3.1415925, ALU.min, ALU.max))
            v.tensor_scalar(bsc[:, :], bn[:, 3, :], BN_EPS, None, ALU.add).then_inc(s_set, 1)
            dve.wait_ge(s_scl, 1)
            lk(v.tensor_tensor(bsc[:, :], bn[:, 0, :], bsh[:, :], ALU.mult))
            lk(v.tensor_tensor(bsh[:, :], bn[:, 2, :], bsc[:, :], ALU.mult))
            lk(v.tensor_tensor(bsh[:, :], bn[:, 1, :], bsh[:, :], ALU.subtract))
            lk(v.tensor_copy(skv[0:DV, :], bsc[0:DV, 7:8]))
            lk(v.tensor_scalar(w1n, w1n, bsc[:, 0:1], None, ALU.mult))
            for oc in range(CC):
                lk(v.tensor_scalar(w3n[:, oc * P:(oc + 1) * P], w3n[:, oc * P:(oc + 1) * P], bsc[:, 3 + oc:4 + oc],
                                   None, ALU.mult))
            lk(v.tensor_scalar(wqn, wqn, bsc[0:64, 1:2], None, ALU.mult))
            lk(v.tensor_scalar(wkvn, wkvn, skv, None, ALU.mult))
            v.tensor_copy(tvb, bsh[0:DV, 7:8].broadcast_to([DV, P])).then_inc(s_set, 1)

            dve.wait_ge(s_trig, 1)
            lk(v.tensor_scalar(ang, angn, -1.0, None, ALU.mult))
            sn, cs, ns = angn[:, 0:18], angn[:, 18:36], ang[:, 0:18]
            for m, (bit, on, off) in enumerate(((gits, sn, cs), (gits, cs, ns), (bits, ns, cs), (bits, cs, sn))):
                lo = 0 if m < 2 else NQ
                lk(v.tensor_scalar(nbit[:, :, :].rearrange("p c q -> p (c q)"),
                                   bit.rearrange("p c q -> p (c q)"), -1.0, 1.0, ALU.mult, ALU.add))
                for kc in range(CC):
                    lk(v.tensor_tensor(al[:, m, kc, :], bit[:, kc, :], on[:, lo:lo + NQ], ALU.mult))
                    lk(v.tensor_tensor(nbit[:, kc, :], nbit[:, kc, :], off[:, lo:lo + NQ], ALU.mult))
                    lk(v.tensor_tensor(al[:, m, kc, :], al[:, m, kc, :], nbit[:, kc, :], ALU.add))
            for mat, dest in ((0, m0), (1, g1)):
                for kc in range(CC):
                    a = lambda q: al[:, 2 * mat, kc, q:q + 1]
                    b_ = lambda q: al[:, 2 * mat + 1, kc, q:q + 1]
                    cur = dbl[0]
                    lk(v.tensor_copy(cur[:, 0:1], a(0)))
                    lk(v.tensor_copy(cur[:, 1:2], b_(0)))
                    for q in range(1, NQ):
                        n = 1 << q
                        nxt = dest[:, kc, :] if q == NQ - 1 else dbl[q % 2]
                        if mat == 0:
                            o = nxt[:, 0:2 * n].rearrange("p (m i) -> p m i", i=2)
                            lk(v.tensor_scalar(o[:, :, 0], cur[:, 0:n], a(q), None, ALU.mult))
                            lk(v.tensor_scalar(o[:, :, 1], cur[:, 0:n], b_(q), None, ALU.mult))
                        else:
                            o = nxt[:, 0:2 * n].rearrange("p (m i) -> p m i", i=4)
                            i_ = cur[:, 0:n].rearrange("p (m i) -> p m i", i=2)
                            lk(v.tensor_scalar(o[:, :, 0:4:3], i_, a(q), None, ALU.mult))
                            lk(v.tensor_scalar(o[:, :, 1:3], i_, b_(q), None, ALU.mult))
                        cur = nxt
            v.memset(st[:, 0, 0, 0:1], 0.0).then_inc(s_set, 1)

            v3 = ep.rearrange("p (r c) -> p r c", r=EPR)
            lk(v.tensor_copy(v3[:, 3:3 + R, 4:4 + R], embn.rearrange("p (r c) -> p r c", r=R)))
            split(v, lk, ep, er, ehp)
            pick(v, lk, er, ehp, ep8)
            v8 = ep8.rearrange("p (r c) -> p r c", r=EPR)
            for oy in range(4):
                for ox in range(4):
                    for c in range(3):
                        o = e8[:, (oy * 4 + ox) * 3 + c, :].rearrange("p (d r m) -> p d r m", d=WCD, r=WROWS)
                        r0 = WROWS * c - oy + 3
                        src = bass.AP(v8.tensor, v8.offset + r0 * EPC + 3 - ox,
                                      [list(v8.ap[0]), [4, WCD], [EPC, WROWS], [1, WCM]])
                        v.tensor_copy(o, src)
            dve.wait_ge(s_spe, 2)
            for jc in range(CC):
                v.tensor_copy(ut[:, jc, :], (CO + VO)[jc][:, :]).then_inc(s_co if jc < 2 else s_vev, 1)

            def gcoef(b, final=None, final2=None):
                n = [0]

                def lg(ins):
                    n[0] += 1
                    link(ins, s_dc, NG * b + n[0])

                def ready(ins, s, k):
                    link(ins, s, k)

                G = lambda i: g[:, i, :]
                mv = g[:, 0:2, :].rearrange("p a b -> p (a b)")
                mean, var = mv[:, 0:8:2], mv[:, 1:8:2]
                dve.wait_ge(s_bs, NU * (b + 1))
                v.memset(G(27), 0.0)
                for oc in range(CC):
                    ins = v.bn_aggr(mv[:, 2 * oc:2 * oc + 2], st[:, oc, :, :].rearrange("p u s -> p (u s)"))
                ready(ins, s_gd, 8 * b + 1)
                dve.wait_ge(s_gp, 8 * b + 1)
                lg(v.tensor_copy(G(27), SM[:, 0:4]))
                lg(v.tensor_tensor(G(2), mean, G(27), ALU.subtract))
                lg(v.tensor_tensor(G(3), G(2), G(2), ALU.mult))
                ready(v.tensor_tensor(G(3), G(3), var, ALU.add), s_gd, 8 * b + 2)
                dve.wait_ge(s_gp, 8 * b + 2)
                v.tensor_scalar(G(4), SM[:, 4:8], GN_EPS0, None, ALU.add).then_inc(s_gv, 1)
                dve.wait_ge(s_gl, 2 * b + 1)
                lg(v.tensor_tensor(G(6), G(2), G(5), ALU.mult))
                ready(v.tensor_tensor(G(7), G(6), G(6), ALU.mult), s_gd, 8 * b + 3)
                if final:
                    final()
                dve.wait_ge(s_gp, 8 * b + 3)
                lg(v.tensor_copy(G(8), SM[:, 8:12]))
                ready(v.tensor_tensor(G(9), G(8), G(8), ALU.mult), s_gd, 8 * b + 4)
                dve.wait_ge(s_gp, 8 * b + 4)
                lg(v.reciprocal(g[0:NQ, 10, 0:1], SM[0:NQ, 13:14]))
                ready(v.tensor_tensor(g[0:NQ, 11, 0:1], SM[0:NQ, 12:13], g[0:NQ, 10, 0:1], ALU.mult), s_gd, 8 * b + 5)
                dve.wait_ge(s_gp, 8 * b + 5)
                v.tensor_tensor(G(12), SM[:, 14:18], fcb_s[:, :], ALU.add).then_inc(s_gx, 1)
                dve.wait_ge(s_ge, b + 1)
                lg(v.tensor_scalar(G(13), G(13), 1.0, None, ALU.add))
                lg(v.reciprocal(G(14), G(13)))
                lg(v.tensor_tensor(G(15), G(14), G(5), ALU.mult))
                lg(v.tensor_scalar(G(16), G(15), 1.0, None, ALU.add))
                lg(v.scalar_tensor_tensor(G(21), G(27), -1.0, G(15), ALU.mult, ALU.mult))
                lg(v.tensor_tensor(G(17), G(14), G(6), ALU.mult))
                ready(v.tensor_tensor(G(17), G(17), mean, ALU.add), s_gd, 8 * b + 6)
                lg(v.tensor_tensor(G(19), G(16), G(16), ALU.mult))
                lg(v.tensor_tensor(G(19), G(19), var, ALU.mult))
                dve.wait_ge(s_gp, 8 * b + 6)
                lg(v.tensor_copy(G(18), SM[:, 18:22]))
                lg(v.tensor_tensor(G(20), G(17), G(18), ALU.subtract))
                lg(v.tensor_tensor(G(20), G(20), G(20), ALU.mult))
                ready(v.tensor_tensor(G(20), G(20), G(19), ALU.add), s_gd, 8 * b + 7)
                dve.wait_ge(s_gp, 8 * b + 7)
                v.tensor_scalar(G(22), SM[:, 22:26], GN_EPS0, None, ALU.add).then_inc(s_gv, 1)
                lg(v.tensor_tensor(G(24), G(21), G(18), ALU.subtract))
                dve.wait_ge(s_gl, 2 * b + 2)
                lg(v.tensor_tensor(G(24), G(24), G(26), ALU.mult))
                lg(v.tensor_tensor(G(23), G(16), G(26), ALU.mult))
                lg(v.tensor_tensor(G(25), G(24), bsh[:, 3:7], ALU.add))
                lg(v.tensor_tensor(G(25), G(25), G(21), ALU.add))
                for oc in range(CC):
                    ins = v.tensor_scalar(w1s[:, oc, :], w1t[:, oc, :], g[:, 23, oc:oc + 1], None, ALU.mult)
                ready(ins, s_gd, 8 * b + 8)
                if final2:
                    final2()
                dve.wait_ge(s_gp, 8 * b + 8)
                v.tensor_tensor(bias1[:, :], SM[:, 26:27], bsh[:, 0:1], ALU.add).then_inc(s_gb, 1)
                assert n[0] == NG, n

            def stats(b, k):
                for oc in range(CC):
                    ins = v.bn_stats(st[:, oc, k, :], xs(b, k, oc))
                ins.then_inc(s_bs, 1)

            def final(b, u, par, ocs=range(CC)):
                U = b * NU + u
                for oc in ocs:
                    dve.wait_ge(s_c3, 4 * U + oc + 1)
                    dve.wait_ge(s_fin, 4 * U + oc + 1)
                    tt = t[:, oc % 2, :]
                    link(v.scalar_tensor_tensor(tt, xs(b, u, oc), coef[:, 0, oc:oc + 1], CO[oc % 2][:, :],
                                                ALU.mult, ALU.add), s_co, 4 * U + oc + 3)
                    v.tensor_scalar(tt, tt, coef[:, 1, oc:oc + 1], coef[:, 2, oc:oc + 1], ALU.add, ALU.max
                                    ).then_inc(s_t, 1)

            def pair(b, a):
                pi = b * PAIRS + a
                for i in range(2):
                    n = 8 * a + 4 * i
                    kv = PB[i][:, 0:192].rearrange("p (n c) -> p n c", c=48)
                    dve.wait_ge(s_kv, 2 * pi + i + 1)
                    v.tensor_tensor(vt[:, bass.ds(n, 4), :], kv[:, :, 0:DV],
                                    bvb[:, :].unsqueeze(1).broadcast_to([P, 4, DV]), ALU.add)
                    mx = kmx[:, bass.ds(n, 4)]
                    link(v.reduce_max(mx, kv[:, :, DV:48], AXX), s_km, 2 * pi + i + 1)
                    v.tensor_tensor(kt[:, bass.ds(n, 4), :], kv[:, :, DV:48],
                                    mx.unsqueeze(2).broadcast_to([P, 4, DK]), ALU.subtract).then_inc(s_kvev, 1)

            def move_coef(b):
                dve.wait_ge(s_fin, 2 + 4 * NU * b)
                for i, k in enumerate((26, 25, 21)):
                    last = v.tensor_copy(coef[:, i, :], g[:, k, :])
                last.then_inc(s_cf, 1)

            def phase_a(b, prev):
                if not prev:
                    with dve.Fori(0, PAIRS) as a:
                        pair(b, a)
                    move_coef(b)
                else:
                    for a in range(PAIRS):
                        pair(b, a)
                        if a < 3:
                            final(b - 1, LATE[a][0], LATE[a][0] % 2, LATE[a][1:])
                    move_coef(b)
                dve.wait_ge(s_ex, PAIRS * (b + 1))
                link(v.reduce_sum(ksum[:, :], kt[:, :, :], AXX), s_sc, 2 * b + 1)
                link(v.reciprocal(ksum[:, :], ksum[:, :]), s_sc, 2 * b + 2)
                v.tensor_tensor(kt[:, :, :], kt[:, :, :], ksum[:, :].unsqueeze(2).broadcast_to([P, 32, DK]),
                                ALU.mult).then_inc(s_kn, 1)

            def content(b):
                n = [0]
                dve.wait_ge(s_cf, b + 1)

                def ll(ins):
                    n[0] += 1
                    link(ins, s_lc, NL * b + n[0])

                dve.wait_ge(s_cl, 2 * b + 1)
                v.tensor_copy(cls[:, :], SM[0:DK, 32:64]).then_inc(s_clc, 1)
                dve.wait_ge(s_cl, 2 * b + 2)
                ll(v.tensor_copy(clf[:, 0, :], SM[:, 64:96]))
                split(v, ll, clf[:, 0, :], clf[:, 1, :], [clh[:, i, :] for i in range(3)])
                pick(v, ll, clf[:, 1, :], [clh[:, i, :] for i in range(3)], cl8[:, :], (s_clc, 1))
                assert n[0] == NL, n

            def sample(b, last):
                content(b)
                if not last:
                    for k in range(2):
                        dve.wait_ge(s_x[k], 16 * (b * 4 + 5))
                        stats(b + 1, k)
                with dve.Fori(1, 3) as w:
                    for i in range(2):
                        final(b, 2 * w + i - 2, i)
                        if not last:
                            dve.wait_ge(s_x[i], 16 * (b * 4 + 5 + w))
                            for oc in range(CC):
                                ins = v.bn_stats(st[:, oc, bass.ds(2 * w + i, 1), :].rearrange("p u s -> p (u s)"),
                                                 xs(b + 1, 2 * w + i, oc))
                            ins.then_inc(s_bs, 1)
                final(b, 4, 0)
                if last:
                    final(b, 5, 1)
                else:
                    for k in (6, 7):
                        dve.wait_ge(s_x[k - 6], 16 * (b * 4 + 8))
                        stats(b + 1, k)
                    gcoef(b + 1, lambda: final(b, 5, 1), lambda: final(b, 6, 0, range(2)))
                if last:
                    final(b, 6, 0)

            v.memset(winf, 0.0).then_inc(s_wz, 1)
            for k in range(NU):
                dve.wait_ge(s_x[k % 2], 16 * (k // 2 + 1))
                stats(0, k)
            gcoef(0)
            phase_a(0, False)
            with dve.Fori(0, NB - 1) as b:
                sample(b, False)
                phase_a(b + 1, True)
            sample(NB - 1, True)
            final(NB - 1, NU - 1, 1)

        @block.gpsimd
        def _(pool):
            v = nc.gpsimd

            def link(ins, s, n):
                ins.then_inc(s, 1)
                pool.wait_ge(s, n)

            for s, dst, src in zip((*s_st, *s_st), (gavg_s, fcb_s, mask_s, rep_s), (gavg, fcb, mask, rep)):
                pool.dma_start(dst[:, :], src).then_inc(s, 16)
            v.memset(zero_s[:, :], 0.0)
            link(v.memset(half[:, :], -0.5), s_fin, 1)
            pool.wait_ge(s_set, 2)
            v.tensor_tensor(bsh[:, :], bsc[:, :], half[:, :], ALU.pow).then_inc(s_scl, 1)
            v.memset(qf[:, 0:1], 0.0).then_inc(s_fin, 1)

            def root(b, k):
                pool.wait_ge(s_gv, 2 * b + k + 1)
                v.tensor_tensor(g[:, 26 if k else 5, :], g[:, 22 if k else 4, :], half[:, 0:4], ALU.pow
                                ).then_inc(s_gl, 1)

            def q_parts(b, a):
                pi = b * PAIRS + a
                pool.wait_ge(s_qf, pi + 1)
                pool.wait_ge(s_qw, 32 * pi)
                n, zeros = [0], zero_s[:, 0:1].broadcast_to([P, 512])

                def lp(ins):
                    n[0] += 1
                    link(ins, s_pc, 5 * pi + n[0])

                lp(v.tensor_tensor(qp[:, 0, :], qf[:, :], zeros, ALU.add))
                lp(v.tensor_tensor(qf[:, :], qf[:, :], qp[:, 0, :], ALU.subtract))
                lp(v.tensor_tensor(qp[:, 1, :], qf[:, :], zeros, ALU.add))
                lp(v.tensor_tensor(qf[:, :], qf[:, :], qp[:, 1, :], ALU.subtract))
                v.tensor_tensor(qp[:, 2, :], qf[:, :], zeros, ALU.add).then_inc(s_pc, 1)

            def final(b, u, par, cnt, ocs=range(CC)):
                U = b * NU + u
                for oc in ocs:
                    pool.wait_ge(s_t, 4 * U + oc + 1)
                    o = xs(b, u, oc)
                    ins = v.tensor_tensor(o, o, t[:, oc % 2, :], ALU.add)
                    ins.then_inc(s_fin, 1)
                if CC - 1 in ocs:
                    pool.wait_ge(s_fin, 2 + 4 * (U + 1))
                    pool.wait_ge(s_st[par], 16 * (cnt + 2))
                    pool.dma_start(dram_unit(out_v, b, u), xslot(b, u)).then_inc(s_st[par], 16)

            def phase_a(b, prev):
                if not prev:
                    q_parts(b, 0)
                    with pool.Fori(1, PAIRS) as a:
                        q_parts(b, a)
                else:
                    for a in range(PAIRS):
                        q_parts(b, a)
                        if a < 3:
                            final(b - 1, LATE[a][0], LATE[a][0] % 2, (b - 1) * 4 + 3, LATE[a][1:])

            def sample(b, last):
                with pool.Fori(1, 3) as w:
                    final(b, 2 * w - 2, 0, b * 4 + w - 1)
                    final(b, 2 * w - 1, 1, b * 4 + w - 1)
                final(b, 4, 0, b * 4 + 2)
                if not last:
                    root(b + 1, 0)
                final(b, 5, 1, b * 4 + 2)
                if not last:
                    root(b + 1, 1)
                final(b, 6, 0, b * 4 + 3, range(CC) if last else range(2))

            root(0, 0)
            root(0, 1)
            phase_a(0, False)
            with pool.Fori(0, NB - 1) as b:
                sample(b, False)
                phase_a(b + 1, True)
            sample(NB - 1, True)
            final(NB - 1, NU - 1, 1, (NB - 1) * 4 + 3)
    return nc


LATE = ((NU - 2, 2, 3), (NU - 1, 0, 1), (NU - 1, 2, 3))
NG = 22
NL = 8


def split(v, link, f, r, parts):
    link(v.tensor_copy(parts[0], f))
    link(v.tensor_tensor(f, f, parts[0], ALU.subtract))
    link(v.tensor_copy(parts[1], f))
    link(v.tensor_tensor(f, f, parts[1], ALU.subtract))
    link(v.tensor_copy(parts[2], f))


def kernel(**inputs):
    import concourse.bacc as bacc
    from concourse.bass_utils import run_bass_kernel_spmd

    a = {k: np.asarray(w) for k, w in inputs.items()}
    l1 = lambda n: a["L1_conv_" + n]
    kh = lambda w: w.reshape(HD, DK, -1).swapaxes(0, 1).reshape(w.shape)
    vh = lambda w: w.reshape(HD, DV, -1).swapaxes(0, 1).reshape(w.shape)
    rows = lambda n: np.stack([l1("bn1_" + n), np.tile(kh(l1("bnq_" + n)), 2), vh(l1("bn2_" + n)),
                               *l1("bn3_" + n).reshape(CC, P), np.tile(l1("bnv_" + n), 4)], axis=1)
    k = np.arange(C).reshape(CC, P).T
    bit = lambda i: ((i[:, :, None] >> np.arange(NQ - 1, -1, -1)) & 1).astype(np.float32)
    rowsq = np.arange(P)
    emb_part = np.array([0, 1, 2, 0, 1, 2, 0, 1])[rowsq // DK]
    consts = {
        "kbit": bit(k), "gbit": bit(k ^ (k >> 1)), "sign": 1 - 2 * bit(k),
        "ident": np.eye(P, dtype=np.float32),
        "gavg": (rowsq[:, None] // GRP == rowsq // GRP).astype(np.float32) / GRP,
        "mask": (emb_part[:, None] == np.arange(3)).astype(np.float32),
        "rep": (rowsq % DK == np.arange(DK)[:, None]).astype(np.float32),
    }
    arrays = {
        "x": a["x"].reshape(NB, C, HW),
        "bnp": np.stack([rows("g"), rows("b"), rows("m"), rows("v")], axis=1),
        "w1": l1("conv1_w"), "w3": vh(l1("conv3_w").T).T, "wq": kh(l1("q_w")),
        "wkv": np.concatenate([l1("v_w"), l1("k_w")]),
        "emb": np.tile(l1("emb").reshape(DK, R * R), (P // DK, 1)),
        "qpar": np.broadcast_to(a["L0_conv_q_params"].reshape(1, 2 * NQ), (P, 2 * NQ)),
        "fcw": a["L0_conv_fc_w"].T, "fcb": a["L0_conv_fc_b"].reshape(CC, P).T,
    } | consts
    arrays = {n: np.ascontiguousarray(w) for n, w in arrays.items()}
    nc = bacc.Bacc("TRN2", target_bir_lowering=False, num_devices=1)
    args = {n: nc.dram_tensor("in_" + n, w.shape, mybir.dt.from_np(w.dtype), kind="ExternalInput").ap()
            for n, w in arrays.items()}
    out = nc.dram_tensor("out", (NB, C, HW), F32, kind="ExternalOutput").ap()
    build(nc, **args, out=out)
    r = run_bass_kernel_spmd(nc, [{"in_" + n: w for n, w in arrays.items()}], core_ids=[0])
    return r.results[0]["out"].reshape(NB, C, 64, 64)
```

```python
from contextlib import ExitStack

import concourse.bass as bass
import concourse.mybir as mybir
import numpy as np

F32 = mybir.dt.float32
BF16 = mybir.dt.bfloat16
ALU = mybir.AluOpType
ACT = mybir.ActivationFunctionType
AXX = mybir.AxisListType.X

P = 128
NB, C, HW = 32, 512, 4096
CC = C // P
GRP = 16
NU, UN = 8, 512
PAIRS = NU // 2
SLOTS = 12
SLOT = CC * UN
WD = 128
HD, DK, DV, R = 4, 16, 32, 15
NQ = 9
WROWS, WCM, WCD = 6, 4, 5
WP = WROWS * WCM * WCD
VROWS, NXB = 78, 16
VROW = WCM * NXB * DV
EPR, EPC = 21, 24
NP = 12
GN_EPS0 = 1e-5
BN_EPS = 1e-5
QPART = DK * HD * UN
TWO_PI = 6.283185307179586
MAGIC = 12582912.0


def build(nc, x, bnp, w1, w3, wq, wkv, emb, qpar, fcw, fcb, kbit, gbit, sign, ident, gavg, mask, rep, out):
    ctx = ExitStack()
    with ctx:
        def sb(name, shape, dt=F32):
            return ctx.enter_context(nc.sbuf_tensor(name, shape, dt))

        def pb(name):
            return ctx.enter_context(nc.psum_tensor(name, [P, 512], F32))

        def sem(name):
            return ctx.enter_context(nc.semaphore(name))

        vpad = nc.dram_tensor("vpad", [VROWS * VROW], F32, kind="Internal").ap()
        qparts_d = nc.dram_tensor("qparts_d", [NU * 3 * QPART], BF16, kind="Internal").ap()

        zmove = nc.dram_tensor("zmove", [2 * P * 512], F32, kind="Internal").ap()

        xr = sb("xr", [P, SLOTS * SLOT])
        pw = sb("pw", [P, 2, 32, 64])
        win = sb("win", [P, 2, 6 * 512])
        e8 = sb("e8", [P, 48, WP], BF16)
        ut = sb("ut", [P, CC, C])
        h1 = sb("h1", [P, 2, UN])
        qf = sb("qf", [P, UN])
        qp = sb("qp", [P, 3, UN], BF16)
        q8 = sb("q8", [P, 2, HD, UN], BF16)
        z1 = sb("z1", [P, 2, HD, P])
        z = sb("z", [P, 2, UN])
        t = sb("t", [P, CC, UN])
        w1t = sb("w1t", [P, CC, P])
        w1s = sb("w1s", [P, CC, P])
        w3t = sb("w3t", [P, C])
        wqt = sb("wqt", [P, HD * DK])
        wkvt = sb("wkvt", [P, DV + DK])
        bvb = sb("bvb", [P, DV])
        kt = sb("kt", [P, 32, DK])
        kmx = sb("kmx", [P, 32])
        ksum = sb("ksum", [P, 32])
        vt = sb("vt", [P, 32, DV])
        cls = sb("cls", [DK, DV])
        clf = sb("clf", [P, 3, DV])
        clh = sb("clh", [P, 3, DV], BF16)
        cl8 = sb("cl8", [P, DV], BF16)
        st = sb("st", [P, CC, NU, 6])
        g = sb("g", [P, 30, CC])
        coef = sb("coef", [P, 3, CC])
        bias1 = sb("bias1", [P, 1])
        bn = sb("bn", [P, 4, 8])
        bsc = sb("bsc", [P, 8])
        bsh = sb("bsh", [P, 8])
        half = sb("half", [P, 8])
        zero_s = sb("zero_s", [P, 1])
        fcw_s = sb("fcw_s", [NQ, C])
        fcb_s = sb("fcb_s", [P, CC])
        sign_s = sb("sign_s", [NQ, C], BF16)
        gavg_s = sb("gavg_s", [P, P])
        mask_s = sb("mask_s", [P, 3])
        rep_s = sb("rep_s", [DK, P])
        ones9 = sb("ones9", [P, NQ])

        pwf = pw[:, :, :, :].rearrange("p a b c -> p (a b c)")
        winf = win[:, :, :].rearrange("p a b -> p (a b)")
        m0 = pwf[:, 0:2048].rearrange("p (c j) -> p c j", c=CC)
        g1 = pwf[:, 2048:4096].rearrange("p (c i) -> p c i", c=CC)
        id_s = winf[:, 3072:3072 + P]
        signn = winf[0:NQ, 3328:3328 + C]
        w1n, w3n = winf[:, 0:512], winf[:, 512:1024]
        wqn, wkvn = winf[0:64, 1024:1152], winf[0:48, 1152:1280]
        ep = winf[:, 1280:1280 + EPR * EPC]
        er = winf[:, 1792:1792 + EPR * EPC]
        embn = winf[:, 2304:2304 + R * R]
        tvb = winf[0:DV, 2560:2560 + P]
        skv = winf[0:48, 2688:2689]
        ang = winf[:, 2700:2736]
        angn = winf[:, 2740:2776]
        bits = winf[:, 2780:2780 + 36].rearrange("p (c q) -> p c q", c=CC)
        gits = winf[:, 2820:2820 + 36].rearrange("p (c q) -> p c q", c=CC)
        al = winf[:, 2860:2860 + 4 * 36].rearrange("p (m c q) -> p m c q", m=4, c=CC)
        nbit = winf[:, 3004:3004 + 36].rearrange("p (c q) -> p c q", c=CC)
        sq = h1[0:NQ, 0, :]
        dbl = [w[:, :, :].rearrange("p a (b n) -> p (a b) n", b=2) for w in (h1, z)]
        eh = q8[:, 0, :, :].rearrange("p a b -> p (a b)")
        ehp = [eh[:, i * 512:i * 512 + EPR * EPC] for i in range(3)]
        ep8 = eh[:, 1536:1536 + EPR * EPC]

        PB = [pb(f"PB{i}") for i in range(3)]
        SM = pb("SM")
        VO = [pb(f"VO{i}") for i in range(2)]
        CO = [pb(f"CO{i}") for i in range(2)]

        s_in = sem("s_in")
        s_zero = sem("s_zero")
        s_wz = sem("s_wz")
        s_set = sem("s_set")
        s_scl = sem("s_scl")
        s_trig = sem("s_trig")
        s_spe = sem("s_spe")
        s_x = [sem(f"s_x{i}") for i in range(2)]
        s_st = [sem(f"s_st{i}") for i in range(2)]
        s_bs = sem("s_bs")
        s_gd = sem("s_gd")
        s_gv = sem("s_gv")
        s_gx = sem("s_gx")
        s_gb = sem("s_gb")
        s_gp = sem("s_gp")
        s_gl = sem("s_gl")
        s_ge = sem("s_ge")
        s_dcs = sem("s_dcs")
        s_dc = sem("s_dc")
        s_km = sem("s_km")
        s_conv = sem("s_conv")
        s_h1 = sem("s_h1")
        s_kv = sem("s_kv")
        s_q = sem("s_q")
        s_qf = sem("s_qf")
        s_pc = sem("s_pc")
        s_qw = sem("s_qw")
        s_kvev = sem("s_kvev")
        s_ex = sem("s_ex")
        s_vw = sem("s_vw")
        s_sc = sem("s_sc")
        s_lc = sem("s_lc")
        s_kn = sem("s_kn")
        s_cl = sem("s_cl")
        s_clc = sem("s_clc")
        s_q8 = [sem(f"s_q8{i}") for i in range(2)]
        s_win = [sem(f"s_win{i}") for i in range(2)]
        s_p = sem("s_p")
        s_pev = sem("s_pev")
        s_vst = sem("s_vst")
        s_vo = sem("s_vo")
        s_vev = sem("s_vev")
        s_zd = [sem(f"s_zd{i}") for i in range(2)]
        s_z = [sem(f"s_z{i}") for i in range(2)]
        s_zr = sem("s_zr")
        s_c3 = sem("s_c3")
        s_co = sem("s_co")
        s_t = sem("s_t")
        s_fin = sem("s_fin")
        s_cf = sem("s_cf")

        N_IN = 11
        block = ctx.enter_context(nc.Block())

        def wait_each(eng, *waits):
            values = [n if isinstance(n, int) else eng.snap(eng.to_reg(n)) for _, n in waits]
            for (s, _), n in zip(waits, values):
                eng.wait_ge(s, n)

        def pick(v, link, f, parts, out, last=None):
            link(v.tensor_scalar(f, parts[0], mask_s[:, 0:1], None, ALU.mult))
            link(v.scalar_tensor_tensor(f, parts[1], mask_s[:, 1:2], f, ALU.mult, ALU.add))
            ins = v.scalar_tensor_tensor(out, parts[2], mask_s[:, 2:3], f, ALU.mult, ALU.add)
            if last:
                ins.then_inc(*last)
            else:
                link(ins)

        def xs(b, u, oc):
            return xr[:, bass.ds(((b * NU + u) % SLOTS) * SLOT + oc * UN, UN)]

        def xslot(b, u):
            return xr[:, bass.ds(((b * NU + u) % SLOTS) * SLOT, SLOT)].rearrange("p (c n) -> p c n", c=CC)

        x_v = x.rearrange("b (c p) n -> b p c n", p=P)
        out_v = out.rearrange("b (c p) n -> b p c n", p=P)

        def dram_unit(v, b, u):
            return v[bass.ds(b, 1), :, :, bass.ds(u * UN, UN)].rearrange("b p c n -> (b p) c n")

        @block.sync
        def _(sp):
            for dst, src in ((bn[:, :, :], bnp), (w1n, w1), (w3n.rearrange("p (c v) -> p c v", c=CC),
                             w3.rearrange("(c p) v -> p c v", p=P)), (wqn, wq), (wkvn, wkv), (embn, emb),
                             (ang[:, 0:18], qpar), (ang[:, 18:36], qpar), (bits, kbit), (gits, gbit),
                             (id_s[:, :], ident)):
                sp.dma_start(dst, src).then_inc(s_in, 16)
            for s, dst, src in ((s_z[0], fcw_s[:, :], fcw), (s_z[1], signn, sign),
                                (s_st[0], gavg_s[:, :], gavg), (s_st[1], fcb_s[:, :], fcb),
                                (s_st[0], mask_s[:, :], mask), (s_st[1], rep_s[:, :], rep)):
                sp.dma_start(dst, src).then_inc(s, 16)

            def load_x(b, k, par):
                sp.dma_start(xslot(b, k), dram_unit(x_v, b, k)).then_inc(s_x[par], 16)

            for k in range(NU):
                if k >= 2:
                    sp.wait_ge(s_x[k % 2], 16 * (k // 2))
                load_x(0, k, k % 2)
            sp.wait_ge(s_set, 1)
            flat = t[:, :, :].rearrange("p a b -> p (a b)")
            body = VROWS * VROW // P
            vz = vpad.rearrange("(p n) -> p n", p=P)
            for o in range(0, body, 1024):
                n = min(1024, body - o)
                sp.dma_start(vz[:, o:o + n], flat[:, 0:n]).then_inc(s_zero, 16)
            sp.wait_ge(s_zero, 16 * (-(-body // 1024)))

            def z_load(b, u, par, cnt):
                sp.wait_ge(s_zd[par], 16 * (cnt + 1))
                src = bass.AP(zmove.tensor, par * (P * 512), [[P, P], [DV * 512, 4], [1, P]])
                sp.dma_start(z[:, par, :].rearrange("p (j n) -> p j n", j=4), src).then_inc(s_z[par], 16)

            def q8_load(u, par):
                for lo, n, part in ((0, 3, 0), (48, 3, 1), (96, 2, 2)):
                    src = bass.AP(qparts_d.tensor, u * (3 * QPART) + part * QPART, [[0, n], [HD * UN, DK], [1, HD * UN]])
                    sp.dma_start(q8[lo:lo + DK * n, par, :, :].rearrange("p h n -> p (h n)"), src
                                 ).then_inc(s_q8[par], 16)

            def win_load(u, par, ybs=range(2)):
                dst = win[:, par, :].rearrange("p (c y n) -> p c y n", c=3, y=2)
                for yb in ybs:
                    for cd in range(WCD):
                        lo, hi = max(0, 2 - cd), min(NXB, NXB + 2 - cd)
                        src = bass.AP(vpad.tensor, u * (8 * VROW) + (4 * yb * VROW + (lo + cd - 2) * DV),
                                      [[NXB * DV, WROWS * WCM], [WROWS * VROW, 3], [1, (hi - lo) * DV]])
                        sp.dma_start(dst[cd * 24:cd * 24 + 24, :, yb, lo * DV:hi * DV], src).then_inc(s_win[par], 16)

            def v_store(a):
                dst = bass.AP(vpad.tensor, a * (16 * VROW) + 7 * VROW, [[DV, P], [2 * VROW, 8], [1, DV]])
                sp.dma_start(dst, vt[:, bass.ds(a * 8, 8), :]).then_inc(s_vw, 16)

            def q_store(a):
                for i in range(2):
                    dst = bass.AP(qparts_d.tensor, a * (6 * QPART) + i * 3 * QPART, [[UN, HD * DK], [QPART, 3], [1, UN]])
                    sp.dma_start(dst, qp[64 * i:64 * i + 64, :, :]).then_inc(s_qw, 16)

            def store_v(b, a):
                pi = b * PAIRS + a
                wait_each(sp, (s_vw, 16 * pi), (s_kvev, 2 * (pi + 1)))
                v_store(a)

            def store_q(b, a):
                pi = b * PAIRS + a
                wait_each(sp, (s_qw, 32 * pi), (s_pc, 5 * (pi + 1)))
                q_store(a)

            def pair_stores(b, a):
                store_v(b, a)
                store_q(b, a)

            def stored(b, a):
                wait_each(sp, (s_vw, 16 * (b * PAIRS + a + 1)), (s_qw, 32 * (b * PAIRS + a + 1)))

            def load_first(b, k):
                wait_each(sp, (s_x[k], 16 * PAIRS * b), (s_st[k], 64 * (b - 1) + 16))
                load_x(b, k, k)

            def phase_a(b, prev, ahead=True):
                if prev:
                    sp.wait_ge(s_vev, 2 + b * NU)
                    z_load(b - 1, NU - 1, 1, (b - 1) * 4 + 3)
                pair_stores(b, 0)
                stored(b, 0)
                q8_load(0, 0)
                q8_load(1, 1)
                win_load(0, 0)
                if ahead:
                    load_first(b + 1, 0)
                pair_stores(b, 1)
                stored(b, 1)
                win_load(1, 1)
                if prev:
                    store(b - 1, NU - 2, 0, (b - 1) * 4 + 3)
                if ahead:
                    load_first(b + 1, 1)
                pair_stores(b, 2)
                store_v(b, 3)
                if prev:
                    store(b - 1, NU - 1, 1, (b - 1) * 4 + 3)

            def load_next(b, h, par):
                wait_each(sp, (s_x[par], 16 * (b * 4 + h + 5)), (s_st[par], 16 * (b * 4 + h + 2)))
                load_x(b + 1, 2 * h + 2 + par, par)

            def store(b, u, par, cnt):
                wait_each(sp, (s_fin, 4 + 4 * (b * NU + u + 1)), (s_st[par], 16 * (cnt + 2)))
                sp.dma_start(dram_unit(out_v, b, u), xslot(b, u)).then_inc(s_st[par], 16)

            def unit(b, u, par, cnt, load, ahead=True, early=False, first=False):
                sp.wait_ge(s_vev, 2 + b * NU + u)
                if early:
                    load()
                if ahead:
                    q8_load(u + 1, 1 - par)
                    win_load(u + 1, 1 - par, (0,))
                z_load(b, u - 1, 1 - par, cnt - (1 - par))
                if not first:
                    store(b, u - 2, par, cnt - 1)
                if ahead:
                    win_load(u + 1, 1 - par, (1,))
                if load and not early:
                    load()

            def sample(b, last):
                store_q(b, 3)

                def after_unit_1():
                    stored(b, PAIRS - 1)
                    if not last:
                        load_next(b, 0, 0)

                unit(b, 1, 1, b * 4, after_unit_1, first=True)
                with sp.Fori(1, 3) as w:
                    unit(b, 2 * w, 0, b * 4 + w, None if last else (lambda: load_next(b, w - 1, 1)))
                    unit(b, 2 * w + 1, 1, b * 4 + w, None if last else (lambda: load_next(b, w, 0)))
                unit(b, 6, 0, b * 4 + 3, None if last else (lambda: load_next(b, 2, 1)), early=not last)
                unit(b, 7, 1, b * 4 + 3, None, ahead=False)

            sp.wait_ge(s_wz, 1)
            phase_a(0, False)
            with sp.Fori(0, NB - 2) as b:
                sample(b, False)
                phase_a(b + 1, True)
            sample(NB - 2, False)
            phase_a(NB - 1, True, ahead=False)
            sample(NB - 1, True)
            z_load(NB - 1, NU - 1, 1, (NB - 1) * 4 + 3)
            for par in range(2):
                store(NB - 1, NU - 2 + par, par, (NB - 1) * 4 + 3)
            sp.wait_ge(s_st[0], 16 * (NB * 4 + 2))
            sp.wait_ge(s_st[1], 16 * (NB * 4 + 2))

        @block.tensor
        def _(pe):
            mm = nc.tensor.matmul
            pe.wait_ge(s_set, 3)
            for oc in range(CC):
                nc.tensor.transpose(PB[0][:, oc * P:(oc + 1) * P], w1n[:, oc * P:(oc + 1) * P], id_s[:, :])
            for oc in range(CC):
                nc.tensor.transpose(PB[1][:, oc * P:(oc + 1) * P], w3n[:, oc * P:(oc + 1) * P], id_s[:, :])
            nc.tensor.transpose(PB[2][:, 0:64], wqn, id_s[0:64, 0:64])
            nc.tensor.transpose(PB[2][:, 64:112], wkvn, id_s[0:48, 0:48])
            mm(PB[2][:, 128:160], tvb, id_s[0:DV, 0:DV], start=True, stop=True).then_inc(s_spe, 1)
            pe.wait_ge(s_set, 4)
            for jc in range(CC):
                o = (CO + VO)[jc]
                for kc in range(CC):
                    last = mm(o[:, :], m0[:, kc, jc * P:(jc + 1) * P], g1[:, kc, :], start=kc == 0, stop=kc == CC - 1)
                    if jc == CC - 1 and kc in (1, 2):
                        last.then_inc(s_vst, 1)
            last.then_inc(s_spe, 1)

            def gstep(b, n):
                pe.wait_ge(s_gd, 8 * b + n)
                if n in (1, 2, 6, 7):
                    col, src = {1: (0, 0), 2: (4, 3), 6: (18, 17), 7: (22, 20)}[n]
                    rhs = mean_ap if n == 1 else g[:, src, :]
                    last = mm(SM[:, col:col + 4], gavg_s[:, :], rhs, start=True, stop=True)
                elif n == 3:
                    for jc in range(CC):
                        last = mm(SM[0:NQ, :], g[:, 6, jc:jc + 1].broadcast_to([P, NQ]), ut[:, jc, :],
                                  start=jc == 0, stop=jc == CC - 1)
                elif n == 4:
                    for jc in range(CC):
                        last = mm(SM[0:NQ, 13:14], ones9[:, :], g[:, 7, jc:jc + 1], start=jc == 0, stop=jc == CC - 1)
                elif n == 5:
                    for oc in range(CC):
                        last = mm(SM[:, 14 + oc:15 + oc], fcw_s[:, oc * P:(oc + 1) * P], g[0:NQ, 11, 0:1],
                                  start=True, stop=True)
                else:
                    for oc in range(CC):
                        last = mm(SM[:, 26:27], w1t[:, oc, :], g[:, 24, oc:oc + 1], start=oc == 0, stop=oc == CC - 1)
                last.then_inc(s_gp, 1)

            def conv3(b, u, par, oc):
                U = b * NU + u
                pe.wait_ge(s_zr, U + 1)
                pe.wait_ge(s_co, 4 * U + oc + 1)
                mm(CO[oc % 2][:, :], w3t[:, oc * P:(oc + 1) * P],
                   z[:, par, :].rearrange("p (j y c) -> p y j c", j=4, y=8), start=True, stop=True
                   ).then_inc(s_c3, 1)

            def pair(b, a, co=None):
                pi = b * PAIRS + a
                for i in range(2):
                    if co is not None:
                        pe.wait_ge(s_co, co + i + 1)
                    for k in range(CC):
                        last = mm(CO[i][:, :], w1s[:, k, :], xs(b, 2 * a + i, k), start=k == 0, stop=k == CC - 1)
                    last.then_inc(s_conv, 1)

                def keys_values(i):
                    pe.wait_ge(s_h1, 2 * pi + i + 1)
                    pe.wait_ge(s_kvev, 2 * pi)
                    for n in range(4):
                        last = mm(PB[i][:, n * 48:(n + 1) * 48], h1[:, i, n * P:(n + 1) * P], wkvt[:, :],
                                  start=True, stop=True)
                    last.then_inc(s_kv, 1)

                keys_values(0)
                pe.wait_ge(s_h1, 2 * pi + 2)
                pe.wait_ge(s_qf, pi)
                mm(VO[0][0:64, :], wqt[:, :], h1[:, 0, :], start=True, stop=True)
                mm(VO[0][64:128, :], wqt[:, :], h1[:, 1, :], start=True, stop=True).then_inc(s_q, 1)
                keys_values(1)

            def phase_a(b, prev):
                pe.wait_ge(s_gd, 8 * b + 8)
                if not prev:
                    pair(b, 0)
                    with pe.Fori(1, PAIRS) as a:
                        pair(b, a)
                else:
                    for a in range(PAIRS):
                        done = sum(len(ocs) for k, (_, ocs) in LATE.items() if k < a)
                        pair(b, a, 2 + 4 * (b * NU - 2) + done)
                        if a in LATE:
                            u, ocs = LATE[a]
                            for oc in ocs:
                                conv3(b - 1, u, u % 2, oc)

            def p_bank(b, u, par, c, oy):
                f = 4 * c + oy
                pe.wait_ge(s_pev, NP * (b * NU + u) + f + 1)
                qv = q8[:, par, :, :].rearrange("p h (y r m d) -> p h y r m d", y=2, r=4, m=4)
                for ox in range(4):
                    last = mm(PB[f % 3][0:WP, ox * P:(ox + 1) * P], e8[:, (oy * 4 + ox) * 3 + c, :],
                              qv[:, :, :, oy, ox, :], start=True, stop=True)
                last.then_inc(s_p, 1)

            def v_quarter(b, u, par, c, k):
                U, yb = b * NU + u, k // 2
                if k == 0:
                    pe.wait_ge(s_pev, 3 + NP * U + 4 * c + 4)
                for xl in (2 * (k % 2), 2 * (k % 2) + 1):
                    for j in range(4):
                        xb = 4 * j + xl
                        o = VO[par][32 * j:32 * j + 32, :].rearrange("p (h y r c) -> p h y r c", h=HD, y=2, r=4)
                        last = mm(o[:, :, yb, :, 4 * xl:4 * xl + 4],
                                  win[0:WP, par, ((c * 2 + yb) * 16 + xb) * DV:((c * 2 + yb) * 16 + xb + 1) * DV],
                                  pw[0:WP, (par * 3 + c) % 2, yb * 16 + xb, :],
                                  start=c == 0 and yb == 0 and xl == 0, stop=False, skip_group_check=True)
                if k == 3:
                    last.then_inc(s_vst, 1)

            def content(b, u, par):
                for h in range(HD):
                    for j in range(4):
                        qv = q8[:, par, h, :].rearrange("p (y m d) -> p y d m", y=8, m=4)
                        last = mm(VO[par][32 * j:32 * j + 32, h * P:(h + 1) * P], cl8[:, :],
                                  qv[:, :, 4 * j:4 * j + 4, :], start=False, stop=True, skip_group_check=True)
                last.then_inc(s_vo, 1)

            def unit(b, w, par, between=None, spread=None, steps="", first=False):
                u, cnt = 2 * w + par, b * 4 + w
                U = b * NU + u
                step = lambda k: gstep(b + 1, k) if str(k) in steps else None
                pe.wait_ge(s_q8[par], 48 * (cnt + 1))
                for k in range(4):
                    if first and k < 2:
                        pe.wait_ge(s_kvev, NU * (b + 1) - 1 + k)
                    p_bank(b, u, par, 0, k)
                    if between:
                        between(k)
                step(3)
                p_bank(b, u, par, 1, 0)
                p_bank(b, u, par, 1, 1)
                pe.wait_ge(s_win[par], 160 * (cnt + 1))
                pe.wait_ge(s_vev, U + 1)
                if first:
                    pe.wait_ge(s_qf, PAIRS * (b + 1))
                v_quarter(b, u, par, 0, 0)
                p_bank(b, u, par, 1, 2)
                v_quarter(b, u, par, 0, 1)
                p_bank(b, u, par, 1, 3)
                v_quarter(b, u, par, 0, 2)
                step(4)
                v_quarter(b, u, par, 0, 3)
                if spread:
                    spread()
                for k in range(4):
                    if k == 0:
                        p_bank(b, u, par, 2, 0)
                    if k < 3:
                        p_bank(b, u, par, 2, k + 1)
                    v_quarter(b, u, par, 1, k)
                    if k == 1:
                        step(5)
                v_quarter(b, u, par, 2, 0)
                v_quarter(b, u, par, 2, 1)
                step(6)
                v_quarter(b, u, par, 2, 2)
                v_quarter(b, u, par, 2, 3)
                if spread:
                    pe.wait_ge(s_clc, 2 * b + 2)
                content(b, u, par)
                for k in (1, 2, 7):
                    step(k)

            def sample(b, last):
                def lambdas(k):
                    if k == 3:
                        pe.wait_ge(s_kn, b + 1)
                        for n in range(32):
                            last = mm(SM[0:DK, 32:64], kt[:, n, :], vt[:, n, :], start=n == 0, stop=n == 31)
                        last.then_inc(s_cl, 1)

                def spread():
                    pe.wait_ge(s_clc, 2 * b + 1)
                    mm(SM[:, 64:96], rep_s[:, :], cls[:, :], start=True, stop=True).then_inc(s_cl, 1)

                unit(b, 0, 0, between=lambdas, spread=spread, first=True)
                unit(b, 0, 1)
                with pe.Fori(1, 3) as w:
                    unit(b, w, 0, between=lambda oc: conv3(b, 2 * w - 2, 0, oc))
                    unit(b, w, 1, between=lambda oc: conv3(b, 2 * w - 1, 1, oc))
                unit(b, 3, 0, between=lambda oc: conv3(b, 4, 0, oc), steps="" if last else "12")
                unit(b, 3, 1, between=lambda oc: conv3(b, 5, 1, oc), steps="" if last else "34567")
                conv3(b, 6, 0, 0)
                conv3(b, 6, 0, 1)
                if not last:
                    gstep(b + 1, 8)
                    return
                conv3(b, 6, 0, 2)
                conv3(b, 6, 0, 3)

            mean_ap = g[:, 0:2, :].rearrange("p a b -> p (a b)")[:, 0:8:2]
            for k in range(1, 9):
                gstep(0, k)
            phase_a(0, False)
            with pe.Fori(0, NB - 1) as b:
                sample(b, False)
                phase_a(b + 1, True)
            sample(NB - 1, True)
            for oc in range(CC):
                conv3(NB - 1, NU - 1, 1, oc)

        @block.scalar
        def _(act):
            act.wait_ge(s_set, 2)
            nc.scalar.activation(angn, ang, ACT.Sin).then_inc(s_trig, 1)

            act.wait_ge(s_spe, 1)
            for i, (dst, src) in enumerate(((w1t[:, :, :].rearrange("p c o -> p (c o)"), PB[0][:, :]),
                                            (w3t[:, :], PB[1][:, :]), (wqt[:, :], PB[2][:, 0:64]),
                                            (wkvt[:, :], PB[2][:, 64:112]), (bvb[:, :], PB[2][:, 128:160]))):
                ins = nc.scalar.activation(dst, src, ACT.Copy)
                if i in (0, 1, 4):
                    ins.then_inc(s_pev, 1)

            def z_relu(b, u, par, cnt):
                act.wait_ge(s_z[par], 16 * (cnt + 2))
                nc.scalar.activation(z[:, par, :], z[:, par, :], ACT.Relu, bias=bsh[:, 2:3], scale=bsc[:, 2:3]
                                     ).then_inc(s_zr, 1)

            def scale(b, u, ocs=range(CC)):
                for oc in ocs:
                    nc.scalar.activation(xs(b, u, oc), xs(b, u, oc), ACT.Copy, scale=g[:, 16, oc:oc + 1])

            def pair(b, a, prev, sc=True):
                pi = b * PAIRS + a
                for i in range(2):
                    act.wait_ge(s_conv, 2 * pi + i + 1)
                    nc.scalar.activation(h1[:, i, :].rearrange("p (y m d) -> p y d m", y=8, m=4),
                                         CO[i][:, :].rearrange("p (y d m) -> p y d m", y=8, m=4),
                                         ACT.Relu, bias=bias1[:, :]).then_inc(s_h1, 1)
                act.wait_ge(s_q, pi + 1)
                act.wait_ge(s_pc, 5 * pi)
                nc.scalar.activation(qf[:, :], VO[0][:, :], ACT.Identity, bias=bsh[:, 1:2]).then_inc(s_qf, 1)
                if prev:
                    z_relu(b - 1, NU - 1, 1, (b - 1) * 4 + 3)
                if sc:
                    scale(b, 2 * a)
                    scale(b, 2 * a + 1)
                act.wait_ge(s_kvev, 2 * pi + 2)
                kp = kt[:, bass.ds(a * 8, 8), :]
                nc.scalar.activation(kp, kp, ACT.Exp).then_inc(s_ex, 1)

            def phase_a(b, prev):
                act.wait_ge(s_gb, b + 1)
                pair(b, 0, prev)
                pair(b, 1, False)
                with act.Fori(2, PAIRS) as a:
                    pair(b, a, False, sc=False)

            def z_out(b, u, par):
                act.wait_ge(s_vev, b * NU + u + 3)
                act.dma_start(bass.AP(zmove.tensor, par * (P * 512), [[512, P], [1, 512]]),
                              z1[:, par, :, :].rearrange("p h n -> p (h n)")).then_inc(s_zd[par], 16)

            def p_copy(b, u, par, c, sc=False, late=False):
                U = b * NU + u
                act.wait_ge(s_vst, 3 * U + c + 1)
                for oy in range(4):
                    f = 4 * c + oy
                    act.wait_ge(s_p, NP * U + f + 1)
                    dst = pw[0:WP, (par * 3 + c) % 2, :, :].rearrange("p k (h r o) -> p r o h k", h=HD, r=4)
                    nc.scalar.activation(dst[:, oy], PB[f % 3][0:WP, :].rearrange("p (o h k) -> p o h k", o=4, h=HD),
                                         ACT.Copy).then_inc(s_pev, 1)
                    if late and oy == 1:
                        z_out(b, u - 1, 1 - par)
                    if sc and oy < 2:
                        scale(b, u + 2, (oy,))

            def unit(b, u, par, cnt, zr=True, ge=False, sc=False, late=False):
                U = b * NU + u
                p_copy(b, u, par, 0, sc, late)
                p_copy(b, u, par, 1)
                p_copy(b, u, par, 2)
                if sc:
                    scale(b, u + 2, (2, 3))
                if ge:
                    gate(b + 1)
                if zr:
                    z_relu(b, u - 1, 1 - par, cnt - (1 - par))
                act.wait_ge(s_vo, U + 1)
                act.wait_ge(s_z[par], 16 * (cnt + 1))
                nc.scalar.activation(z1[:, par, :, :].rearrange("p h n -> p (h n)"), VO[par][:, :], ACT.Copy
                                     ).then_inc(s_vev, 1)
                if zr:
                    z_out(b, u, par)

            def gate(b):
                act.wait_ge(s_gx, b + 1)
                nc.scalar.activation(g[:, 13, :], g[:, 12, :], ACT.Exp, scale=-1.0).then_inc(s_ge, 1)

            def sample(b, last):
                unit(b, 0, 0, b * 4, zr=False)
                unit(b, 1, 1, b * 4, late=True)
                with act.Fori(1, 3) as w:
                    for i in range(2):
                        unit(b, 2 * w + i, i, b * 4 + w, sc=True)
                unit(b, 6, 0, b * 4 + 3)
                unit(b, 7, 1, b * 4 + 3, ge=not last)

            gate(0)
            phase_a(0, False)
            with act.Fori(0, NB - 1) as b:
                sample(b, False)
                phase_a(b + 1, True)
            sample(NB - 1, True)
            z_relu(NB - 1, NU - 1, 1, (NB - 1) * 4 + 3)

        @block.vector
        def _(dve):
            v = nc.vector
            set_n = [0]

            def link(ins, s, n):
                ins.then_inc(s, 1)
                dve.wait_ge(s, n)

            def lk(ins):
                set_n[0] += 1
                link(ins, s_dcs, set_n[0])

            def nl(ins):
                set_n[0] += 1
                ins.then_inc(s_dcs, 1)

            v.memset(t[:, :, :], 0.0).then_inc(s_set, 1)
            v.memset(ones9[:, :], 1.0)
            v.memset(ep, 0.0)
            lk(v.memset(skv, 1.0))
            dve.wait_ge(s_in, 16 * N_IN)
            for s, n in zip((*s_st, *s_z), (32, 32, 16, 16)):
                dve.wait_ge(s, n)
            v.tensor_copy(sign_s[:, :], signn)
            lk(v.tensor_scalar(ang[:, 0:18], ang[:, 0:18], 0.5, None, ALU.mult))
            lk(v.tensor_scalar(ang[:, 18:36], ang[:, 18:36], 0.5, TWO_PI / 4, ALU.mult, ALU.add))
            lk(v.tensor_scalar(angn, ang, 1.0 / TWO_PI, MAGIC, ALU.mult, ALU.add))
            lk(v.tensor_scalar(angn, angn, MAGIC, None, ALU.subtract))
            lk(v.scalar_tensor_tensor(ang, angn, -6.28125, ang, ALU.mult, ALU.add))
            lk(v.scalar_tensor_tensor(ang, angn, 6.28125 - TWO_PI, ang, ALU.mult, ALU.add))
            lk(v.tensor_scalar(ang, ang, 3.1415925, -3.1415925, ALU.min, ALU.max))
            v.tensor_scalar(bsc[:, :], bn[:, 3, :], BN_EPS, None, ALU.add).then_inc(s_set, 1)
            dve.wait_ge(s_scl, 1)
            lk(v.tensor_tensor(bsc[:, :], bn[:, 0, :], bsh[:, :], ALU.mult))
            lk(v.tensor_tensor(bsh[:, :], bn[:, 2, :], bsc[:, :], ALU.mult))
            lk(v.tensor_tensor(bsh[:, :], bn[:, 1, :], bsh[:, :], ALU.subtract))
            lk(v.tensor_copy(skv[0:DV, :], bsc[0:DV, 7:8]))
            nl(v.tensor_scalar(w1n, w1n, bsc[:, 0:1], None, ALU.mult))
            for oc in range(CC):
                nl(v.tensor_scalar(w3n[:, oc * P:(oc + 1) * P], w3n[:, oc * P:(oc + 1) * P], bsc[:, 3 + oc:4 + oc],
                                   None, ALU.mult))
            nl(v.tensor_scalar(wqn, wqn, bsc[0:64, 1:2], None, ALU.mult))
            lk(v.tensor_scalar(wkvn, wkvn, skv, None, ALU.mult))
            v.tensor_copy(tvb, bsh[0:DV, 7:8].broadcast_to([DV, P])).then_inc(s_set, 1)

            dve.wait_ge(s_trig, 1)
            lk(v.tensor_scalar(ang, angn, -1.0, None, ALU.mult))
            sn, cs, ns = angn[:, 0:18], angn[:, 18:36], ang[:, 0:18]
            for m, (bit, on, off) in enumerate(((gits, sn, cs), (gits, cs, ns), (bits, ns, cs), (bits, cs, sn))):
                lo = 0 if m < 2 else NQ
                lk(v.tensor_scalar(nbit[:, :, :].rearrange("p c q -> p (c q)"),
                                   bit.rearrange("p c q -> p (c q)"), -1.0, 1.0, ALU.mult, ALU.add))
                for kc in range(CC):
                    nl(v.tensor_tensor(al[:, m, kc, :], bit[:, kc, :], on[:, lo:lo + NQ], ALU.mult))
                    (lk if kc == CC - 1 else nl)(
                        v.tensor_tensor(nbit[:, kc, :], nbit[:, kc, :], off[:, lo:lo + NQ], ALU.mult))
                lk(v.tensor_tensor(al[:, m, :, :], al[:, m, :, :], nbit[:, :, :], ALU.add))
            for mat, dest in ((0, m0), (1, g1)):
                a = lambda kc, q: al[:, 2 * mat, kc, q:q + 1]
                b_ = lambda kc, q: al[:, 2 * mat + 1, kc, q:q + 1]
                for kc in range(CC):
                    nl(v.tensor_copy(dbl[0][:, kc, 0:1], a(kc, 0)))
                    (lk if kc == CC - 1 else nl)(v.tensor_copy(dbl[0][:, kc, 1:2], b_(kc, 0)))
                for q in range(1, NQ):
                    n = 1 << q
                    for kc in range(CC):
                        cur = dbl[(q - 1) % 2][:, kc, :]
                        nxt = dest[:, kc, :] if q == NQ - 1 else dbl[q % 2][:, kc, :]
                        if mat == 0:
                            o = nxt[:, 0:2 * n].rearrange("p (m i) -> p m i", i=2)
                            i_, oa, ob = cur[:, 0:n], o[:, :, 0], o[:, :, 1]
                        else:
                            o = nxt[:, 0:2 * n].rearrange("p (m i) -> p m i", i=4)
                            i_, oa, ob = cur[:, 0:n].rearrange("p (m i) -> p m i", i=2), o[:, :, 0:4:3], o[:, :, 1:3]
                        nl(v.tensor_scalar(oa, i_, a(kc, q), None, ALU.mult))
                        (lk if kc == CC - 1 else nl)(v.tensor_scalar(ob, i_, b_(kc, q), None, ALU.mult))
            v.memset(st[:, 0, 0, 0:1], 0.0).then_inc(s_set, 1)

            v3 = ep.rearrange("p (r c) -> p r c", r=EPR)
            lk(v.tensor_copy(v3[:, 3:3 + R, 4:4 + R], embn.rearrange("p (r c) -> p r c", r=R)))
            split(v, lk, ep, er, ehp)
            pick(v, lk, er, ehp, ep8)
            v8 = ep8.rearrange("p (r c) -> p r c", r=EPR)
            for oy in range(4):
                for ox in range(4):
                    for c in range(3):
                        o = e8[:, (oy * 4 + ox) * 3 + c, :].rearrange("p (d r m) -> p d r m", d=WCD, r=WROWS)
                        r0 = WROWS * c - oy + 3
                        src = bass.AP(v8.tensor, v8.offset + r0 * EPC + 3 - ox,
                                      [list(v8.ap[0]), [4, WCD], [EPC, WROWS], [1, WCM]])
                        v.tensor_copy(o, src)
            dve.wait_ge(s_spe, 2)
            for jc in range(CC):
                v.tensor_copy(ut[:, jc, :], (CO + VO)[jc][:, :]).then_inc(s_co if jc < 2 else s_vev, 1)

            def gcoef(b, final=None, final2=None):
                n = [0]

                def lg(ins):
                    n[0] += 1
                    link(ins, s_dc, NG * b + n[0])

                def ready(ins, s, k):
                    link(ins, s, k)

                G = lambda i: g[:, i, :]
                mv = g[:, 0:2, :].rearrange("p a b -> p (a b)")
                mean, var = mv[:, 0:8:2], mv[:, 1:8:2]
                dve.wait_ge(s_bs, NU * (b + 1))
                v.memset(G(27), 0.0)
                for oc in range(CC):
                    ins = v.bn_aggr(mv[:, 2 * oc:2 * oc + 2], st[:, oc, :, :].rearrange("p u s -> p (u s)"))
                ready(ins, s_gd, 8 * b + 1)
                dve.wait_ge(s_gp, 8 * b + 1)
                lg(v.tensor_copy(G(27), SM[:, 0:4]))
                lg(v.tensor_tensor(G(2), mean, G(27), ALU.subtract))
                lg(v.tensor_tensor(G(3), G(2), G(2), ALU.mult))
                ready(v.tensor_tensor(G(3), G(3), var, ALU.add), s_gd, 8 * b + 2)
                dve.wait_ge(s_gp, 8 * b + 2)
                v.tensor_scalar(G(4), SM[:, 4:8], GN_EPS0, None, ALU.add).then_inc(s_gv, 1)
                dve.wait_ge(s_gl, 2 * b + 1)
                lg(v.tensor_tensor(G(6), G(2), G(5), ALU.mult))
                ready(v.tensor_tensor(G(7), G(6), G(6), ALU.mult), s_gd, 8 * b + 3)
                if final:
                    final()
                dve.wait_ge(s_gp, 8 * b + 3)
                lg(v.tensor_tensor(sq, SM[0:NQ, :], sign_s[:, :], ALU.mult))
                ready(v.tensor_tensor_reduce(sq, sq, SM[0:NQ, :], 1.0, 0.0, ALU.mult, ALU.add, g[0:NQ, 9, 0:1]),
                      s_gd, 8 * b + 4)
                dve.wait_ge(s_gp, 8 * b + 4)
                lg(v.reciprocal(g[0:NQ, 10, 0:1], SM[0:NQ, 13:14]))
                ready(v.tensor_tensor(g[0:NQ, 11, 0:1], g[0:NQ, 9, 0:1], g[0:NQ, 10, 0:1], ALU.mult), s_gd, 8 * b + 5)
                dve.wait_ge(s_gp, 8 * b + 5)
                v.tensor_tensor(G(12), SM[:, 14:18], fcb_s[:, :], ALU.add).then_inc(s_gx, 1)
                dve.wait_ge(s_ge, b + 1)
                lg(v.tensor_scalar(G(13), G(13), 1.0, None, ALU.add))
                lg(v.reciprocal(G(14), G(13)))
                lg(v.tensor_tensor(G(15), G(14), G(5), ALU.mult))
                lg(v.tensor_scalar(G(16), G(15), 1.0, None, ALU.add))
                lg(v.scalar_tensor_tensor(G(21), G(27), -1.0, G(15), ALU.mult, ALU.mult))
                lg(v.tensor_tensor(G(17), G(14), G(6), ALU.mult))
                ready(v.tensor_tensor(G(17), G(17), mean, ALU.add), s_gd, 8 * b + 6)
                lg(v.tensor_tensor(G(19), G(16), G(16), ALU.mult))
                lg(v.tensor_tensor(G(19), G(19), var, ALU.mult))
                dve.wait_ge(s_gp, 8 * b + 6)
                lg(v.tensor_copy(G(18), SM[:, 18:22]))
                lg(v.tensor_tensor(G(20), G(17), G(18), ALU.subtract))
                lg(v.tensor_tensor(G(20), G(20), G(20), ALU.mult))
                ready(v.tensor_tensor(G(20), G(20), G(19), ALU.add), s_gd, 8 * b + 7)
                dve.wait_ge(s_gp, 8 * b + 7)
                v.tensor_scalar(G(22), SM[:, 22:26], GN_EPS0, None, ALU.add).then_inc(s_gv, 1)
                lg(v.tensor_tensor(G(24), G(21), G(18), ALU.subtract))
                dve.wait_ge(s_gl, 2 * b + 2)
                lg(v.tensor_tensor(G(24), G(24), G(26), ALU.mult))
                lg(v.tensor_tensor(G(23), G(16), G(26), ALU.mult))
                lg(v.tensor_tensor(G(25), G(24), bsh[:, 3:7], ALU.add))
                lg(v.tensor_tensor(G(25), G(25), G(21), ALU.add))
                for oc in range(CC):
                    ins = v.tensor_scalar(w1s[:, oc, :], w1t[:, oc, :], g[:, 23, oc:oc + 1], None, ALU.mult)
                ready(ins, s_gd, 8 * b + 8)
                if final2:
                    final2()
                dve.wait_ge(s_gp, 8 * b + 8)
                v.tensor_tensor(bias1[:, :], SM[:, 26:27], bsh[:, 0:1], ALU.add).then_inc(s_gb, 1)
                assert n[0] == NG, n

            def stats(b, k):
                for oc in range(CC):
                    ins = v.bn_stats(st[:, oc, k, :], xs(b, k, oc))
                ins.then_inc(s_bs, 1)

            def final(b, u, ocs=range(CC)):
                U = b * NU + u
                for oc in ocs:
                    dve.wait_ge(s_c3, 4 * U + oc + 1)
                    dve.wait_ge(s_fin, 4 * U + oc + 1)
                    tt = t[:, oc, :]
                    link(v.scalar_tensor_tensor(tt, xs(b, u, oc), coef[:, 0, oc:oc + 1], CO[oc % 2][:, :],
                                                ALU.mult, ALU.add), s_co, 4 * U + oc + 3)
                    v.tensor_scalar(tt, tt, coef[:, 1, oc:oc + 1], coef[:, 2, oc:oc + 1], ALU.add, ALU.max
                                    ).then_inc(s_t, 1)

            def pair(b, a):
                pi = b * PAIRS + a
                for i in range(2):
                    n = 8 * a + 4 * i
                    kv = PB[i][:, 0:192].rearrange("p (n c) -> p n c", c=48)
                    dve.wait_ge(s_kv, 2 * pi + i + 1)
                    v.tensor_tensor(vt[:, bass.ds(n, 4), :], kv[:, :, 0:DV],
                                    bvb[:, :].unsqueeze(1).broadcast_to([P, 4, DV]), ALU.add)
                    mx = kmx[:, bass.ds(n, 4)]
                    link(v.reduce_max(mx, kv[:, :, DV:48], AXX), s_km, 2 * pi + i + 1)
                    v.tensor_tensor(kt[:, bass.ds(n, 4), :], kv[:, :, DV:48],
                                    mx.unsqueeze(2).broadcast_to([P, 4, DK]), ALU.subtract).then_inc(s_kvev, 1)

            def move_coef(b):
                for i, k in enumerate((26, 25, 21)):
                    last = v.tensor_copy(coef[:, i, :], g[:, k, :])
                last.then_inc(s_cf, 1)

            def phase_a(b, prev):
                if not prev:
                    with dve.Fori(0, PAIRS) as a:
                        pair(b, a)
                else:
                    for a in range(PAIRS):
                        pair(b, a)
                        if a in LATE and a < PAIRS - 1:
                            final(b - 1, *LATE[a])
                dve.wait_ge(s_ex, PAIRS * (b + 1))
                link(v.reduce_sum(ksum[:, :], kt[:, :, :], AXX), s_sc, 2 * b + 1)
                link(v.reciprocal(ksum[:, :], ksum[:, :]), s_sc, 2 * b + 2)
                v.tensor_tensor(kt[:, :, :], kt[:, :, :], ksum[:, :].unsqueeze(2).broadcast_to([P, 32, DK]),
                                ALU.mult).then_inc(s_kn, 1)
                if prev:
                    final(b - 1, *LATE[PAIRS - 1])
                    dve.wait_ge(s_t, 4 * NU * b)
                move_coef(b)

            def content(b):
                n = [0]
                dve.wait_ge(s_cf, b + 1)

                def ll(ins):
                    n[0] += 1
                    link(ins, s_lc, NL * b + n[0])

                dve.wait_ge(s_cl, 2 * b + 1)
                v.tensor_copy(cls[:, :], SM[0:DK, 32:64]).then_inc(s_clc, 1)
                dve.wait_ge(s_cl, 2 * b + 2)
                ll(v.tensor_copy(clf[:, 0, :], SM[:, 64:96]))
                split(v, ll, clf[:, 0, :], clf[:, 1, :], [clh[:, i, :] for i in range(3)])
                pick(v, ll, clf[:, 1, :], [clh[:, i, :] for i in range(3)], cl8[:, :], (s_clc, 1))
                assert n[0] == NL, n

            def sample(b, last):
                content(b)
                if not last:
                    for k in range(2):
                        dve.wait_ge(s_x[k], 16 * (b * 4 + 5))
                        stats(b + 1, k)
                with dve.Fori(1, 3) as w:
                    for i in range(2):
                        final(b, 2 * w + i - 2)
                        if not last:
                            dve.wait_ge(s_x[i], 16 * (b * 4 + 5 + w))
                            for oc in range(CC):
                                ins = v.bn_stats(st[:, oc, bass.ds(2 * w + i, 1), :].rearrange("p u s -> p (u s)"),
                                                 xs(b + 1, 2 * w + i, oc))
                            ins.then_inc(s_bs, 1)
                final(b, 4)
                if last:
                    final(b, 5)
                else:
                    for k in (6, 7):
                        dve.wait_ge(s_x[k - 6], 16 * (b * 4 + 8))
                        stats(b + 1, k)
                    gcoef(b + 1, lambda: final(b, 5), lambda: final(b, 6, range(2)))
                if last:
                    final(b, 6)

            v.memset(winf, 0.0).then_inc(s_wz, 1)
            for k in range(NU):
                dve.wait_ge(s_x[k % 2], 16 * (k // 2 + 1))
                stats(0, k)
            gcoef(0)
            phase_a(0, False)
            with dve.Fori(0, NB - 1) as b:
                sample(b, False)
                phase_a(b + 1, True)
            sample(NB - 1, True)
            final(NB - 1, NU - 1)

        @block.gpsimd
        def _(pool):
            v = nc.gpsimd

            def link(ins, s, n):
                ins.then_inc(s, 1)
                pool.wait_ge(s, n)

            v.memset(zero_s[:, :], 0.0).then_inc(s_fin, 1)
            link(v.memset(half[:, :], -0.5), s_fin, 2)
            pool.wait_ge(s_set, 2)
            v.tensor_tensor(bsh[:, :], bsc[:, :], half[:, :], ALU.pow).then_inc(s_scl, 1)
            for i in range(2):
                v.memset(qf[:, i:i + 1], 0.0).then_inc(s_fin, 1)

            def root(b, k):
                pool.wait_ge(s_gv, 2 * b + k + 1)
                v.tensor_tensor(g[:, 26 if k else 5, :], g[:, 22 if k else 4, :], half[:, 0:4], ALU.pow
                                ).then_inc(s_gl, 1)

            def q_parts(b, a):
                pi = b * PAIRS + a
                pool.wait_ge(s_qf, pi + 1)
                pool.wait_ge(s_qw, 32 * pi)
                n, zeros = [0], zero_s[:, 0:1].broadcast_to([P, 512])

                def lp(ins):
                    n[0] += 1
                    link(ins, s_pc, 5 * pi + n[0])

                lp(v.tensor_tensor(qp[:, 0, :], qf[:, :], zeros, ALU.add))
                lp(v.tensor_tensor(qf[:, :], qf[:, :], qp[:, 0, :], ALU.subtract))
                lp(v.tensor_tensor(qp[:, 1, :], qf[:, :], zeros, ALU.add))
                lp(v.tensor_tensor(qf[:, :], qf[:, :], qp[:, 1, :], ALU.subtract))
                v.tensor_tensor(qp[:, 2, :], qf[:, :], zeros, ALU.add).then_inc(s_pc, 1)

            def final(b, u, ocs=range(CC)):
                U = b * NU + u
                for oc in ocs:
                    pool.wait_ge(s_t, 4 * U + oc + 1)
                    o = xs(b, u, oc)
                    ins = v.tensor_tensor(o, o, t[:, oc, :], ALU.add)
                    ins.then_inc(s_fin, 1)

            def phase_a(b, prev):
                if not prev:
                    q_parts(b, 0)
                    with pool.Fori(1, PAIRS) as a:
                        q_parts(b, a)
                else:
                    for a in range(PAIRS - 1):
                        q_parts(b, a)
                        if a in LATE:
                            final(b - 1, *LATE[a])
                    final(b - 1, *LATE[PAIRS - 1])
                    q_parts(b, PAIRS - 1)

            def sample(b, last):
                with pool.Fori(1, 3) as w:
                    final(b, 2 * w - 2)
                    final(b, 2 * w - 1)
                final(b, 4)
                if not last:
                    root(b + 1, 0)
                final(b, 5)
                if not last:
                    root(b + 1, 1)
                final(b, 6, range(CC) if last else range(2))

            root(0, 0)
            root(0, 1)
            phase_a(0, False)
            with pool.Fori(0, NB - 1) as b:
                sample(b, False)
                phase_a(b + 1, True)
            sample(NB - 1, True)
            final(NB - 1, NU - 1)
    return nc


LATE = {0: (NU - 2, (2, 3)), 1: (NU - 1, (0, 1)), 3: (NU - 1, (2, 3))}
NG = 22
NL = 8


def split(v, link, f, r, parts):
    link(v.tensor_copy(parts[0], f))
    link(v.tensor_tensor(f, f, parts[0], ALU.subtract))
    link(v.tensor_copy(parts[1], f))
    link(v.tensor_tensor(f, f, parts[1], ALU.subtract))
    link(v.tensor_copy(parts[2], f))


def kernel(**inputs):
    import concourse.bacc as bacc
    from concourse.bass_utils import run_bass_kernel_spmd

    a = {k: np.asarray(w) for k, w in inputs.items()}
    l1 = lambda n: a["L1_conv_" + n]
    kh = lambda w: w.reshape(HD, DK, -1).swapaxes(0, 1).reshape(w.shape)
    vh = lambda w: w.reshape(HD, DV, -1).swapaxes(0, 1).reshape(w.shape)
    rows = lambda n: np.stack([l1("bn1_" + n), np.tile(kh(l1("bnq_" + n)), 2), vh(l1("bn2_" + n)),
                               *l1("bn3_" + n).reshape(CC, P), np.tile(l1("bnv_" + n), 4)], axis=1)
    k = np.arange(C).reshape(CC, P).T
    bit = lambda i: ((i[:, :, None] >> np.arange(NQ - 1, -1, -1)) & 1).astype(np.float32)
    rowsq = np.arange(P)
    emb_part = np.array([0, 1, 2, 0, 1, 2, 0, 1])[rowsq // DK]
    consts = {
        "kbit": bit(k), "gbit": bit(k ^ (k >> 1)), "sign": (1 - 2 * bit(np.arange(C)[None])[0]).T,
        "ident": np.eye(P, dtype=np.float32),
        "gavg": (rowsq[:, None] // GRP == rowsq // GRP).astype(np.float32) / GRP,
        "mask": (emb_part[:, None] == np.arange(3)).astype(np.float32),
        "rep": (rowsq % DK == np.arange(DK)[:, None]).astype(np.float32),
    }
    arrays = {
        "x": a["x"].reshape(NB, C, HW),
        "bnp": np.stack([rows("g"), rows("b"), rows("m"), rows("v")], axis=1),
        "w1": l1("conv1_w"), "w3": vh(l1("conv3_w").T).T, "wq": kh(l1("q_w")),
        "wkv": np.concatenate([l1("v_w"), l1("k_w")]),
        "emb": np.tile(l1("emb").reshape(DK, R * R), (P // DK, 1)),
        "qpar": np.broadcast_to(a["L0_conv_q_params"].reshape(1, 2 * NQ), (P, 2 * NQ)),
        "fcw": a["L0_conv_fc_w"].T, "fcb": a["L0_conv_fc_b"].reshape(CC, P).T,
    } | consts
    arrays = {n: np.ascontiguousarray(w) for n, w in arrays.items()}
    nc = bacc.Bacc("TRN2", target_bir_lowering=False, num_devices=1)
    args = {n: nc.dram_tensor("in_" + n, w.shape, mybir.dt.from_np(w.dtype), kind="ExternalInput").ap()
            for n, w in arrays.items()}
    out = nc.dram_tensor("out", (NB, C, HW), F32, kind="ExternalOutput").ap()
    build(nc, **args, out=out)
    r = run_bass_kernel_spmd(nc, [{"in_" + n: w for n, w in arrays.items()}], core_ids=[0])
    return r.results[0]["out"].reshape(NB, C, 64, 64)
```
